# Optimizing a Trainium2 kernel written in Bass

```python
import numpy as np
import jax
import jax.numpy as jnp

def _softmax(x, axis=-1):
    return jax.nn.softmax(x, axis=axis)

def _gelu(x):
    return jax.nn.gelu(x, approximate=True)

def _silu(x):
    return jax.nn.silu(x)

def _sigmoid(x):
    return jax.nn.sigmoid(x)

def _layernorm(x, axis=-1, eps=1e-05):
    m = jnp.mean(x, axis=axis, keepdims=True)
    v = jnp.var(x, axis=axis, keepdims=True)
    return (x - m) / jnp.sqrt(v + eps)

def _scatter_add(tgt, idx, src, axis=0):
    return tgt.at[idx].add(src)

def _segment_sum(src, seg, n):
    return jax.ops.segment_sum(src, seg, n)
kernel_name = 'mk_cond_resid_d1_seqx_r4_ac04f9'

def setup_inputs(seed: int=0):
    np.random.seed(seed)
    _w = jnp.asarray

    def _rec_inputs():
        import jax
        import jax.numpy as jnp
        _rk = jax.random.key(seed)
        x = -0.0003929 + 0.9999 * jax.random.normal(jax.random.fold_in(_rk, 1), (32, 64, 1024), jnp.float32)
        _lenS = 64 - jax.random.randint(jax.random.fold_in(_rk, 7), (32,), 0, max(1, 64 // 4) + 1, jnp.int32)
        _lenS2 = 64 - jax.random.randint(jax.random.fold_in(_rk, 8), (32,), 0, max(1, 64 // 4) + 1, jnp.int32)
        cond_512 = 0.00782532 + 1.00527 * jax.random.normal(jax.random.fold_in(_rk, 11), (32, 128), jnp.float32)
        return (x, cond_512)
    x, cond_512 = _rec_inputs()

    def _L0_cond_setup():
        import jax, jax.numpy as jnp
        from jax import lax
        import numpy as np
        CIN, COUT, K, STYLE_DIM = (64, 64, 3, 128)
        N_LAYERS = 4
        TYPES = ('same', 'upsample', 'same', 'downsample')
        SCALE = 1.0 / float(np.sqrt(CIN * K ** 2))
        EPS = 1e-08
        _BK = np.array([1.0, 3.0, 3.0, 1.0], dtype=np.float32)
        BLUR_K = _BK / _BK.sum()

        def _blur(x, kern, pad):
            B, C, _ = x.shape
            xp = jnp.pad(x, ((0, 0), (0, 0), (pad[0], pad[1])))
            w = jnp.broadcast_to(kern.astype(x.dtype)[None, None, :], (C, 1, kern.shape[0]))
            return lax.conv_general_dilated(xp, w, (1,), 'VALID', feature_group_count=C, dimension_numbers=('NCH', 'OIH', 'NCH'))

        def _conv_same(x, w):
            p = (K - 1) // 2
            return lax.conv_general_dilated(x[None], w, (1,), [(p, p)], dimension_numbers=('NCH', 'OIH', 'NCH'))[0]

        def _conv_down(x, w):
            return lax.conv_general_dilated(x[None], w, (2,), 'VALID', dimension_numbers=('NCH', 'OIH', 'NCH'))[0]

        def _conv_up(x, w_t):
            return lax.conv_transpose(x[None], w_t, (2,), 'VALID', dimension_numbers=('NCH', 'IOH', 'NCH'), transpose_kernel=True)[0]

        def _layer(x, style, w, b, mw, mb, typ):
            s = style @ mw.T + mb
            weight = SCALE * w * s[:, None, :, None]
            demod = lax.rsqrt(jnp.sum(weight * weight, axis=(2, 3)) + EPS)
            weight = weight * demod[:, :, None, None]
            blur_k = jnp.asarray(BLUR_K)
            if typ == 'same':
                out = jax.vmap(_conv_same)(x, weight) + b[None, :, None]
            elif typ == 'upsample':
                out = jax.vmap(_conv_up)(x, weight.transpose(0, 2, 1, 3)) + b[None, :, None]
                out = _blur(out, 2.0 * blur_k, (1, 1))
            elif typ == 'downsample':
                xb = _blur(x, blur_k, (2, 2))
                out = jax.vmap(_conv_down)(xb, weight) + b[None, :, None]
            else:
                raise NotImplementedError(typ)
            return out
        key = jax.random.key(seed)
        ks = jax.random.split(key, 6)
        B, L = (16, 1024)
        return {'x': jax.random.normal(ks[0], (B, CIN, L), dtype=jnp.float32), 'style': jax.random.normal(ks[1], (B, STYLE_DIM), dtype=jnp.float32), 'weights': jax.random.normal(ks[2], (N_LAYERS, COUT, CIN, K), dtype=jnp.float32), 'biases': jax.random.normal(ks[3], (N_LAYERS, COUT), dtype=jnp.float32) * 0.1, 'mod_w': jax.random.normal(ks[4], (N_LAYERS, CIN, STYLE_DIM), dtype=jnp.float32) / np.sqrt(STYLE_DIM), 'mod_b': 1.0 + 0.1 * jax.random.normal(ks[5], (N_LAYERS, CIN), dtype=jnp.float32)}
    _L0_cond_all = _L0_cond_setup()
    _L0_cond_in = {k: v for k, v in _L0_cond_all.items() if k in ('weights', 'biases', 'mod_w', 'mod_b')}
    del _L0_cond_all
    return {'x': x, 'cond_512': cond_512, 'L0_cond_weights': _L0_cond_in['weights'], 'L0_cond_biases': _L0_cond_in['biases'], 'L0_cond_mod_w': _L0_cond_in['mod_w'], 'L0_cond_mod_b': _L0_cond_in['mod_b']}

def reference(x, cond_512, L0_cond_weights, L0_cond_biases, L0_cond_mod_w, L0_cond_mod_b):
    import jax
    import jax.numpy as jnp

    def _L0_cond_ref(x, style, weights, biases, mod_w, mod_b):
        import jax, jax.numpy as jnp
        from jax import lax
        import numpy as np
        CIN, COUT, K, STYLE_DIM = (64, 64, 3, 128)
        N_LAYERS = 4
        TYPES = ('same', 'upsample', 'same', 'downsample')
        SCALE = 1.0 / float(np.sqrt(CIN * K ** 2))
        EPS = 1e-08
        _BK = np.array([1.0, 3.0, 3.0, 1.0], dtype=np.float32)
        BLUR_K = _BK / _BK.sum()

        def _blur(x, kern, pad):
            B, C, _ = x.shape
            xp = jnp.pad(x, ((0, 0), (0, 0), (pad[0], pad[1])))
            w = jnp.broadcast_to(kern.astype(x.dtype)[None, None, :], (C, 1, kern.shape[0]))
            return lax.conv_general_dilated(xp, w, (1,), 'VALID', feature_group_count=C, dimension_numbers=('NCH', 'OIH', 'NCH'))

        def _conv_same(x, w):
            p = (K - 1) // 2
            return lax.conv_general_dilated(x[None], w, (1,), [(p, p)], dimension_numbers=('NCH', 'OIH', 'NCH'))[0]

        def _conv_down(x, w):
            return lax.conv_general_dilated(x[None], w, (2,), 'VALID', dimension_numbers=('NCH', 'OIH', 'NCH'))[0]

        def _conv_up(x, w_t):
            return lax.conv_transpose(x[None], w_t, (2,), 'VALID', dimension_numbers=('NCH', 'IOH', 'NCH'), transpose_kernel=True)[0]

        def _layer(x, style, w, b, mw, mb, typ):
            s = style @ mw.T + mb
            weight = SCALE * w * s[:, None, :, None]
            demod = lax.rsqrt(jnp.sum(weight * weight, axis=(2, 3)) + EPS)
            weight = weight * demod[:, :, None, None]
            blur_k = jnp.asarray(BLUR_K)
            if typ == 'same':
                out = jax.vmap(_conv_same)(x, weight) + b[None, :, None]
            elif typ == 'upsample':
                out = jax.vmap(_conv_up)(x, weight.transpose(0, 2, 1, 3)) + b[None, :, None]
                out = _blur(out, 2.0 * blur_k, (1, 1))
            elif typ == 'downsample':
                xb = _blur(x, blur_k, (2, 2))
                out = jax.vmap(_conv_down)(xb, weight) + b[None, :, None]
            else:
                raise NotImplementedError(typ)
            return out
        out = x
        for i, typ in enumerate(TYPES):
            out = _layer(out, style, weights[i], biases[i], mod_w[i], mod_b[i], typ)
        return out
    x = x + _L0_cond_ref(x, cond_512, L0_cond_weights, L0_cond_biases, L0_cond_mod_w, L0_cond_mod_b)
    return x

_drawn_inputs = setup_inputs


def setup_inputs(seed=0):
    import zlib

    import numpy as np

    out = dict(_drawn_inputs(seed))
    spreads = {}
    factors = {}
    for name, (base, spread) in spreads.items():
        noise = np.random.default_rng([zlib.crc32(name.encode()), seed]).standard_normal(out[name].shape)
        drawn = base * np.exp(spread * noise) if base else spread * noise
        out[name] = jnp.asarray(drawn.astype(out[name].dtype))
    for name, factor in factors.items():
        out[name] = (out[name] * factor).astype(out[name].dtype)
    return out
```

```python
from contextlib import ExitStack

import concourse.bass as bass
from concourse import mybir

F32 = mybir.dt.float32
F32R = mybir.dt.float32r
ACT = mybir.ActivationFunctionType
ALU = mybir.AluOpType
AX_X = mybir.AxisListType.X

P = 128
PASSES = ((0, 0), (0, 1), (1, 0))
V_S0, V_A0, V_B0, V_E1, V_E2, V_D3, V_C, V_SB1, V_SB2, NVEC = range(10)


def modulated_conv_kernel(nc, x, cond, weights, biases, mod_w, mod_b, out):
    B, C, L = x.shape
    LAYERS, _, _, K = weights.shape
    STYLE = cond.shape[1]
    PAIRS = B // 2
    HALF = L // 2
    SCALE2 = 1.0 / (C * K * K)
    SCALE = float(SCALE2 ** 0.5)
    EPS = 1e-8
    BP = B + 2
    XW = L + 12
    NXS = HALF + 6
    NJ = (HALF + 4) // 2
    NM = HALF - 2
    NR, NA, NH = 5, 4, 7
    EDGE = 3

    ctx = ExitStack()
    with ctx:
        def sb(name, shape, dt=F32):
            return ctx.enter_context(nc.sbuf_tensor(name, shape, dt))

        def ps(name, shape):
            return ctx.enter_context(nc.psum_tensor(name, shape, F32))

        def sem(name):
            return ctx.enter_context(nc.semaphore(name))

        def per_slot(make, name, *a):
            return [make(f"{name}{s}", *a) for s in range(2)]

        ident = sb("ident", [P, P])
        wn = sb("wn", [P, LAYERS, C, K])
        mwn = sb("mwn", [P, 2, STYLE])
        cn = sb("cn", [B, STYLE])
        bias = sb("bias", [P, LAYERS])
        mbias = sb("mbias", [P, LAYERS])
        mwT = sb("mwT", [P, LAYERS, 2, C])
        cT = sb("cT", [P, B])
        style = sb("style", [P, LAYERS, B])
        style2 = sb("style2", [P, LAYERS, B])
        wsq = sb("wsq", [C, LAYERS, C, K])
        wsum = sb("wsum", [C, LAYERS, C])
        wsumT = sb("wsumT", [C, LAYERS, 2, C])
        dt_ = sb("dt_", [P, LAYERS, B])
        dq = sb("dq", [P, LAYERS, B])
        dr = sb("dr", [P, LAYERS, B])
        da = sb("da", [P, LAYERS, B])
        dm = sb("dm", [P, LAYERS, B])
        vec = sb("vec", [P, NVEC, BP])
        blur = sb("blur", [P, 2, 8, C])
        F_st = sb("F_st", [P, 3, C])
        V_st = sb("V_st", [P, 2, P])
        G_mv = sb("G_mv", [P, NA, C])
        w0T = sb("w0T", [P, K, C])
        w0_st = sb("w0_st", [P, 2, P])
        w0_hl = sb("w0_hl", [P, 2, 2, P], F32R)
        y_st = sb("y_st", [C, 6, C])
        z_st = sb("z_st", [P, 3, P])
        o_st = sb("o_st", [P, 3, C])
        xe = sb("xe", [C, 2, B, 8])
        xse = sb("xse", [C, 2, B, 8])
        x0e = sb("x0e", [C, 2, B, 7])
        ye = sb("ye", [P, 2, B, 6])
        ze = sb("ze", [P, 2, B, 5])
        yc = sb("yc", [P, B])
        zc = sb("zc", [P, B])
        oe = sb("oe", [C, B, 2, EDGE])
        xin = per_slot(sb, "xin", [P, XW])
        xs = per_slot(sb, "xs", [P, 2, NXS], F32R)
        xr = per_slot(sb, "xr", [C, L])
        x0f = per_slot(sb, "x0f", [P, 2, NJ])
        x0 = per_slot(sb, "x0", [P, 2, 2 * NJ], F32R)
        A_sb = per_slot(sb, "A_sb", [P, NA, C])
        R_sb = per_slot(sb, "R_sb", [P, NR, C])
        H_hl = sb("H_hl", [P, 2, NH, C], F32R)
        H_st = per_slot(sb, "H_st", [P, 2, NH + 1, C], F32R)
        ot = per_slot(sb, "ot", [C, L])
        p_l0 = per_slot(ps, "p_l0", [P, 2, 512])
        p_out = per_slot(ps, "p_out", [P, 512])
        p_R = ps("p_R", [P, 512])
        p_H = ps("p_H", [P, 512])

        zeroed = sem("zeroed")
        ident_made = sem("ident_made")
        w_loaded = sem("w_loaded")
        s_loaded = sem("s_loaded")
        e_loaded = sem("e_loaded")
        x_loaded = per_slot(sem, "x_loaded")
        put = {n: sem(f"put_{n}") for n in ("styleT", "w02T", "wsumT", "style", "demod", "GT", "FT",
                                            "x0e", "ye", "ze", "oe")}
        made = {n: sem(f"made_{n}") for n in ("wsum", "styleT", "style2", "blur", "dt", "vec", "weights",
                                              "xse", "x0e", "ye", "ze", "c", "oe")}
        dve_step = sem("dve_step")
        sqrt_done = sem("sqrt_done")
        xh_made = per_slot(sem, "xh_made")
        xl_made = per_slot(sem, "xl_made")
        xr_made = per_slot(sem, "xr_made")
        l0_done = per_slot(sem, "l0_done")
        x0_evac = per_slot(sem, "x0_evac")
        x0h_made = per_slot(sem, "x0h_made")
        x0l_made = per_slot(sem, "x0l_made")
        A_made = per_slot(sem, "A_made")
        R_done = per_slot(sem, "R_done")
        R_evac = per_slot(sem, "R_evac")
        H_done = sem("H_done")
        Hh_made = sem("Hh_made")
        Hl_made = sem("Hl_made")
        H_placed = per_slot(sem, "H_placed")
        main_done = per_slot(sem, "main_done")
        out_made = per_slot(sem, "out_made")
        edge_put = per_slot(sem, "edge_put")
        stored = per_slot(sem, "stored")

        def wait(eng, s, value):
            if not isinstance(value, int) or value > 0:
                eng.wait_ge(s, value)

        def col(v, n, lo=0, hi=P):
            return vec[lo:hi, v, bass.ds(n, 1)]

        block = ctx.enter_context(nc.Block())

        @block.gpsimd
        def _(pool):
            for s in range(2):
                pool.memset(xin[s][:, 0:2], 0.0).then_inc(zeroed, 1)
                pool.memset(xin[s][:, L:XW], 0.0).then_inc(zeroed, 1)
            pool.memset(xe[:], 0.0).then_inc(zeroed, 1)
            pool.memset(ident[:], 0.0).then_inc(zeroed, 1)
            pool.wait_ge(zeroed, 6)
            pool.affine_select(out=ident[:], in_=ident[:], compare_op=ALU.not_equal, fill=1.0, base=0,
                               pattern=[[-1, P]], channel_multiplier=1).then_inc(ident_made, 1)
            for t in (blur, V_st, w0_st, z_st, x0e, ye, ze, vec):
                pool.memset(t[:], 0.0).then_inc(zeroed, 1)
            count = 14
            for s in range(2):
                for rows, block in ((slice(0, C), NH), (slice(C, P), 0)):
                    pool.wait_ge(zeroed, count)
                    pool.memset(H_st[s][rows, :, block, :].bitcast(F32), 0.0).then_inc(zeroed, 1)
                    count += 1
            pool.wait_ge(zeroed, count)
            pool.wait_ge(made["oe"], 1)
            def put_edges(p):
                for s in range(2):
                    wait(pool, stored[s], 16 * p)
                    n = p * 2 + s
                    pool.tensor_copy(ot[s][:, 0:EDGE], oe[:, bass.ds(n, 1), 0, :].rearrange("c a n -> c (a n)"))\
                        .then_inc(edge_put[s], 1)
                    pool.tensor_copy(ot[s][:, L - EDGE:L], oe[:, bass.ds(n, 1), 1, :].rearrange("c a n -> c (a n)"))\
                        .then_inc(edge_put[s], 1)

            put_edges(0)
            with pool.Fori(1, PAIRS) as p:
                put_edges(p)

        @block.sync
        def _(sp):
            sp.dma_start(mwn[:], mod_w.rearrange("(t l) c s -> (l c) t s", t=2)).then_inc(s_loaded, 16)
            sp.dma_start(cn[:], cond).then_inc(s_loaded, 16)
            for h in range(2):
                rows = slice(h * C, h * C + C)
                sp.dma_start(wn[rows], weights.rearrange("l o i k -> o l i k")).then_inc(w_loaded, 16)
                sp.dma_start(mbias[rows], mod_b.rearrange("l c -> c l"), allow_slow_non_contiguous=True).then_inc(s_loaded, 16)
                sp.dma_start(bias[rows], biases.rearrange("l c -> c l"), allow_slow_non_contiguous=True).then_inc(s_loaded, 16)

            def load(s, p):
                n = p * 2 + s
                wait(sp, xl_made[s], p)
                wait(sp, xr_made[s], p)
                src = x[bass.ds(n, 1), :, :].rearrange("a c l -> (a c) l")
                sp.dma_start(xin[s][0:C, 2:2 + L], src).then_inc(x_loaded[s], 16)
                sp.dma_start(xin[s][C:P, 1:1 + L], src).then_inc(x_loaded[s], 16)

            def place_H(p):
                wait(sp, Hl_made, p + 1)
                wait(sp, main_done[1], p)
                sp.dma_start(H_st[1][0:C, :, 0:NH, :].bitcast(F32), H_hl[C:P].bitcast(F32)).then_inc(H_placed[1], 16)
                sp.dma_start(H_st[1][C:P, :, 1:NH + 1, :].bitcast(F32), H_hl[C:P].bitcast(F32)).then_inc(H_placed[1], 16)

            def store(s, p):
                n = p * 2 + s
                wait(sp, out_made[s], 2 * (p + 1))
                wait(sp, edge_put[s], 2 * (p + 1))
                dst = out[bass.ds(n, 1), :, :].rearrange("a c l -> (a c) l")
                sp.dma_start(dst, ot[s][:]).then_inc(stored[s], 16)

            sp.wait_ge(zeroed, 5)
            load(0, 0)
            load(1, 0)
            sp.dma_start(xe[:, 0, :, 1:8], x[:, :, 0:7].rearrange("b c n -> c b n")).then_inc(e_loaded, 16)
            sp.dma_start(xe[:, 1, :, 0:7], x[:, :, L - 7:L].rearrange("b c n -> c b n")).then_inc(e_loaded, 16)
            place_H(0)
            load(0, 1)
            load(1, 1)

            def turn(p):
                store(0, p)
                load(0, p + 2)
                place_H(p + 1)
                store(1, p)
                load(1, p + 2)

            turn(0)
            with sp.Fori(1, PAIRS - 2) as p:
                turn(p)
            p = PAIRS - 2
            store(0, p)
            place_H(p + 1)
            store(1, p)
            for s in range(2):
                store(s, PAIRS - 1)
            for s in range(2):
                sp.wait_ge(stored[s], 16 * PAIRS)

        @block.tensor
        def _(pe):
            pe.wait_ge(ident_made, 1)
            pe.wait_ge(s_loaded, 16 * 6)
            for t in range(2):
                pe.transpose(p_l0[0][:, 0, t * P:(t + 1) * P], mwn[:, t, :], ident[:])
            pe.transpose(p_l0[0][:, 0, 2 * P:2 * P + B], cn[:], ident[0:B, 0:B]).then_inc(put["styleT"], 1)
            pe.wait_ge(w_loaded, 32)
            for m, l in enumerate((0, 2)):
                for k in range(K):
                    c0 = (m * K + k) * C
                    for h in range(2):
                        src = wn[0:C, l, :, k]
                        ins = pe.matmul(p_out[0][h * C:(h + 1) * C, c0:c0 + C], src, ident[0:C, 0:C],
                                        start=True, stop=True)
            ins.then_inc(put["w02T"], 1)
            pe.wait_ge(made["wsum"], 1)
            for l in range(LAYERS):
                ins = pe.transpose(p_l0[1][0:C, 0, l * C:(l + 1) * C], wsum[:, l, :], ident[0:C, 0:C])
            ins.then_inc(put["wsumT"], 1)
            pe.wait_ge(made["styleT"], 1)
            for l in range(LAYERS):
                ins = pe.matmul(p_l0[0][:, 1, l * B:(l + 1) * B], mwT[:, l].rearrange("p a c -> p (a c)"), cT[:],
                                start=True, stop=True)
            ins.then_inc(put["style"], 1)
            pe.wait_ge(made["style2"], 1)
            for l in range(LAYERS):
                ins = pe.matmul(p_l0[1][:, 1, l * B:(l + 1) * B], wsumT[:, l].rearrange("p a c -> p (a c)"),
                                style2[0:C, l, :], start=True, stop=True)
            ins.then_inc(put["demod"], 1)
            pe.wait_ge(made["blur"], 1)
            for m in range(NA):
                k0 = (NA - 1 - m) * C
                pe.transpose(p_out[1][:, k0:k0 + C], blur[0:C, 1, 2 * m:2 * m + 2, :].rearrange("p t i -> p (t i)"),
                             ident[0:C, 0:C])
            for m in range(3):
                k0 = (NA + m) * C
                ins = pe.transpose(p_out[1][:, k0:k0 + C],
                                   blur[0:C, 1, 2 * m + 1:2 * m + 3, :].rearrange("p t i -> p (t i)"),
                                   ident[0:C, 0:C])
            ins.then_inc(put["GT"], 1)
            for m in range(3):
                ins = pe.transpose(p_R[:, m * C:(m + 1) * C],
                                   blur[0:C, 0, 2 * m + 1:2 * m + 3, :].rearrange("p t i -> p (t i)"),
                                   ident[0:C, 0:C])
            ins.then_inc(put["FT"], 1)

            def compose_R(s, p):
                wait(pe, A_made[s], p + 1)
                if s == 0:
                    wait(pe, R_evac[1], p)
                else:
                    wait(pe, R_evac[0], p + 1)
                for b in range(2):
                    ins = pe.matmul(p_R[:, b * C:(b + NA) * C], V_st[:, b, :],
                                    A_sb[s][:].rearrange("p a c -> p (a c)"), start=(b == 0), stop=(b == 1),
                                    skip_group_check=True)
                ins.then_inc(R_done[s], 1)

            def compose_H(p):
                wait(pe, Hl_made, p)
                wait(pe, R_evac[0], p + 1)
                wait(pe, R_evac[1], p + 1)
                for c in range(3):
                    for s in range(2):
                        ins = pe.matmul(p_H[s * C:(s + 1) * C, c * C:(c + NR) * C], F_st[:, c, :],
                                        R_sb[s][:].rearrange("p a c -> p (a c)"), start=(c == 0), stop=(c == 2),
                                        skip_group_check=True)
                ins.then_inc(H_done, 1)

            def layer0(s, p):
                wait(pe, xl_made[s], p + 1)
                wait(pe, x0_evac[s], p)
                for bank in range(2):
                    for q, (a, b) in enumerate(PASSES):
                        for st in range(2):
                            e0 = bank * NJ + st
                            ins = pe.matmul(p_l0[s][:, bank, 0:NJ], w0_hl[:, a, st, :], xs[s][:, b, e0:e0 + NJ],
                                            start=(q == 0 and st == 0), stop=(q == 2 and st == 1))
                ins.then_inc(l0_done[s], 1)

            def main(s, p):
                if s == 0:
                    wait(pe, H_placed[0], 2 * (p + 1))
                else:
                    wait(pe, H_placed[1], 32 * (p + 1))
                wait(pe, x0l_made[s], p + 1)
                wait(pe, out_made[s], 2 * p)
                for q, (a, b) in enumerate(PASSES):
                    for t in range(4):
                        blk = NH - 1 - 2 * t
                        ins = pe.matmul(p_out[s][:, 0:NM],
                                        H_st[s][:, a, blk:blk + 2, :].rearrange("p a c -> p (a c)"),
                                        x0[s][:, b, t:t + NM], start=(q == 0 and t == 0), stop=(q == 2 and t == 3))
                ins.then_inc(main_done[s], 1)

            pe.wait_ge(made["weights"], 1)
            compose_R(0, 0)
            compose_R(1, 0)
            layer0(0, 0)
            compose_H(0)
            layer0(1, 0)

            pe.wait_ge(made["xse"], 1)
            for k in range(K):
                ins = pe.matmul(p_out[0][0:C, 0:2 * B * 6], w0T[0:C, k, :], xse[:, :, :, k:k + 6],
                                start=(k == 0), stop=(k == K - 1))
            ins.then_inc(put["x0e"], 1)
            pe.wait_ge(made["x0e"], 1)
            for k in range(K):
                c = 4 - 2 * k
                ins = pe.matmul(p_out[1][:, 0:2 * B * 5], y_st[:, c:c + 2, :].rearrange("p a c -> p (a c)"),
                                x0e[:, :, :, k:k + 5], start=(k == 0), stop=(k == K - 1))
            ins.then_inc(put["ye"], 1)
            pe.wait_ge(made["ye"], 1)
            nz = 2 * B * 4
            for k in range(3):
                pe.matmul(p_out[0][:, 0:nz], z_st[:, k, :], ye[:, :, :, k:k + 4], start=(k == 0), stop=(k == 2))
            for k in range(3):
                ins = pe.matmul(p_out[0][:, nz:nz + B], z_st[:, k, :], yc[:], start=(k == 0), stop=(k == 2))
            ins.then_inc(put["ze"], 1)
            pe.wait_ge(made["ze"], 1)
            no = 2 * B * EDGE
            for k in range(3):
                pe.matmul(p_out[1][0:C, 0:no], o_st[:, k, :], ze[:, :, :, k:k + EDGE], start=(k == 0), stop=(k == 2))
            for k in range(3):
                ins = pe.matmul(p_out[1][0:C, no:no + B], o_st[:, k, :], zc[:], start=(k == 0), stop=(k == 2))
            ins.then_inc(put["oe"], 1)
            pe.wait_ge(made["oe"], 1)

            def turn(p):
                compose_R(0, p + 1)
                main(0, p)
                compose_R(1, p + 1)
                layer0(0, p + 1)
                compose_H(p + 1)
                main(1, p)
                layer0(1, p + 1)

            turn(0)
            with pe.Fori(1, PAIRS - 1) as p:
                turn(p)
            main(0, PAIRS - 1)
            main(1, PAIRS - 1)

        @block.scalar
        def _(act):
            act.wait_ge(made["dt"], 1)
            act.activation(dq[:], dt_[:], ACT.Sqrt).then_inc(sqrt_done, 1)
            act.wait_ge(made["vec"], 1)

            def split_x(s, p):
                wait(act, x_loaded[s], 32 * (p + 1))
                wait(act, l0_done[s], p)
                act.activation(xs[s][:, 0, 0:NXS - 1], xin[s][:, 0:2 * NXS - 2:2], ACT.Copy,
                               scale=col(V_S0, p * 2 + s)).then_inc(xh_made[s], 1)

            def evac_R(s, p):
                wait(act, R_done[s], p + 1)
                wait(act, H_done, p)
                act.activation(R_sb[s][:].rearrange("p a c -> p (a c)"), p_R[:, 0:NR * C], ACT.Copy,
                               scale=col(V_E1, p * 2 + s)).then_inc(R_evac[s], 1)

            def evac_x0(s, p):
                wait(act, l0_done[s], p + 1)
                wait(act, x0l_made[s], p)
                n = p * 2 + s
                act.activation(x0f[s][:], p_l0[s][:, :, 0:NJ], ACT.Identity, scale=col(V_A0, n),
                               bias=col(V_B0, n)).then_inc(x0_evac[s], 1)

            def evac_H(p):
                wait(act, H_done, p + 1)
                wait(act, H_placed[0], 2 * p)
                wait(act, H_placed[1], 32 * p)
                act.activation(H_hl[:, 0], p_H[:, 0:NH * C].rearrange("p (a c) -> p a c", c=C), ACT.Copy)\
                   .then_inc(Hh_made, 1)

            def residual(s, p):
                wait(act, out_made[s], 2 * p)
                act.activation(xr[s][:], xin[s][0:C, 2:2 + L], ACT.Identity, bias=col(V_C, p * 2 + s, 0, C))\
                   .then_inc(xr_made[s], 1)

            split_x(0, 0)
            split_x(1, 0)
            evac_R(0, 0)
            evac_R(1, 0)
            evac_x0(0, 0)
            evac_H(0)
            evac_x0(1, 0)
            act.wait_ge(made["c"], 1)
            residual(0, 0)
            residual(1, 0)
            def turn(p):
                split_x(0, p + 1)
                evac_R(0, p + 1)
                split_x(1, p + 1)
                evac_R(1, p + 1)
                residual(0, p + 1)
                evac_x0(0, p + 1)
                evac_H(p + 1)
                evac_x0(1, p + 1)
                residual(1, p + 1)

            turn(0)
            with act.Fori(1, PAIRS - 1) as p:
                turn(p)

        @block.vector
        def _(dve):
            n_step = [0]

            def step(ins, name=None):
                if name:
                    ins.then_inc(made[name], 1)
                    dve.wait_ge(made[name], 1)
                else:
                    n_step[0] += 1
                    ins.then_inc(dve_step, 1)
                    dve.wait_ge(dve_step, n_step[0])

            def tt(o, a, b, op, name=None):
                step(dve.tensor_tensor(o, a, b, op), name)

            def ts(o, a, s1, s2=None, op0=ALU.mult, op1=ALU.bypass, name=None):
                if s2 is None:
                    step(dve.tensor_scalar(o, a, s1, None, op0), name)
                else:
                    step(dve.tensor_scalar(o, a, s1, s2, op0, op1), name)

            def stt(o, a, s1, b, op0, op1, name=None):
                step(dve.scalar_tensor_tensor(out=o, in0=a, scalar=s1, in1=b, op0=op0, op1=op1), name)

            dve.wait_ge(w_loaded, 32)
            tt(wsq[:], wn[0:C], wn[0:C], ALU.mult)
            step(dve.tensor_reduce(wsum[:], wsq[:], AX_X, ALU.add), "wsum")
            dve.wait_ge(put["styleT"], 1)
            for h in range(2):
                ts(mwT[:, :, h, :], p_l0[0][:, 0, 0:2 * P].rearrange("p (l c) -> p l c", c=C), 1.0)
            ts(cT[:], p_l0[0][:, 0, 2 * P:2 * P + B], 1.0, name="styleT")
            dve.wait_ge(put["wsumT"], 1)
            for h in range(2):
                ts(wsumT[:, :, h, :], p_l0[1][0:C, 0, 0:LAYERS * C].rearrange("p (l c) -> p l c", c=C), 1.0)
            dve.wait_ge(s_loaded, 16 * 6)
            dve.wait_ge(put["style"], 1)
            tt(style[:], p_l0[0][:, 1, 0:LAYERS * B].rearrange("p (l b) -> p l b", b=B),
               mbias[:].unsqueeze(2).to_broadcast([P, LAYERS, B]), ALU.add)
            tt(style2[:], style[:], style[:], ALU.mult, "style2")
            dve.wait_ge(zeroed, 18)
            w = [wn[:, 1:4:2, :, k] for k in range(K)]
            u = [blur[:, :, c + 1, :] for c in range(6)]
            ts(u[0], w[0], 1.0)
            ts(u[5], w[2], 1.0)
            stt(u[1], w[0], 3.0, w[1], ALU.mult, ALU.add)
            stt(u[4], w[2], 3.0, w[1], ALU.mult, ALU.add)
            stt(u[2], w[1], 2.0, u[1], ALU.mult, ALU.add)
            stt(u[3], w[1], 2.0, u[4], ALU.mult, ALU.add)
            tt(u[2], u[2], w[2], ALU.add)
            tt(u[3], u[3], w[0], ALU.add, "blur")
            dve.wait_ge(put["demod"], 1)
            ts(dt_[:], p_l0[1][:, 1, 0:LAYERS * B].rearrange("p (l b) -> p l b", b=B), SCALE2, EPS,
               ALU.mult, ALU.add, "dt")
            dve.wait_ge(sqrt_done, 1)
            step(dve.reciprocal(dr[:], dq[:]))
            tt(da[:], dr[:], dr[:], ALU.mult)
            tt(da[:], da[:], dt_[:], ALU.mult)
            ts(da[:], da[:], -0.5 * SCALE, 1.5 * SCALE, ALU.mult, ALU.add)
            tt(dm[:], dr[:], da[:], ALU.mult)
            ts(vec[:, V_S0, 0:B], style[:, 0, :], 1.0)
            tt(vec[:, V_A0, 0:B], dm[:, 1, :], dm[:, 0, :], ALU.mult)
            ts(vec[:, V_B0, 0:B], dm[:, 1, :], bias[:, 0:1])
            tt(vec[:, V_E1, 0:B], style[:, 2, :], style[:, 1, :], ALU.mult)
            tt(vec[:, V_E2, 0:B], style[:, 3, :], dm[:, 2, :], ALU.mult)
            ts(vec[:, V_D3, 0:B], dm[:, 3, :], 1.0)
            ts(vec[:, V_SB1, 0:B], style[:, 2, :], bias[:, 1:2])
            ts(vec[:, V_SB2, 0:B], style[:, 3, :], bias[:, 2:3], name="vec")
            ts(y_st[:], blur[0:C, 0, 1:7, :], 0.25)
            V = [wn[:, 2, :, K - 1 - b] for b in range(K)]
            ts(V_st[0:C, 0, 0:C], V[0][0:C], 1.0)
            ts(V_st[C:P, 0, 0:C], V[1][C:P], 1.0)
            ts(V_st[C:P, 0, C:P], V[0][C:P], 1.0)
            ts(V_st[0:C, 1, 0:C], V[2][0:C], 1.0)
            ts(V_st[0:C, 1, C:P], V[1][0:C], 1.0)
            ts(V_st[C:P, 1, C:P], V[2][C:P], 1.0)
            dve.wait_ge(put["GT"], 1)
            ts(G_mv[:], p_out[1][:, 0:NA * C].rearrange("p (a c) -> p a c", c=C), 0.125)
            ts(o_st[:], p_out[1][:, NA * C:(NA + 3) * C].rearrange("p (a c) -> p a c", c=C), 0.125)
            dve.wait_ge(put["FT"], 1)
            ts(F_st[:], p_R[:, 0:3 * C].rearrange("p (a c) -> p a c", c=C), 0.25)
            wT = p_out[0][:, 0:6 * C].rearrange("p (l k c) -> p l k c", l=2, c=C)
            ts(w0T[:], wT[:, 0], 1.0)
            ts(w0_st[0:C, 0, 0:C], wT[0:C, 0, 0], 1.0)
            ts(w0_st[C:P, 0, 0:C], wT[C:P, 0, 1], 1.0)
            ts(w0_st[C:P, 0, C:P], wT[C:P, 0, 0], 1.0)
            ts(w0_st[0:C, 1, 0:C], wT[0:C, 0, 2], 1.0)
            ts(w0_st[0:C, 1, C:P], wT[0:C, 0, 1], 1.0)
            ts(w0_st[C:P, 1, C:P], wT[C:P, 0, 2], 1.0)
            ts(z_st[C:P, 0, 0:C], wT[C:P, 1, 0], 1.0)
            ts(z_st[0:C, 1, 0:C], wT[0:C, 1, 1], 1.0)
            ts(z_st[0:C, 1, C:P], wT[0:C, 1, 0], 1.0)
            ts(z_st[C:P, 1, 0:C], wT[C:P, 1, 2], 1.0)
            ts(z_st[C:P, 1, C:P], wT[C:P, 1, 1], 1.0)
            ts(z_st[0:C, 2, C:P], wT[0:C, 1, 2], 1.0)
            ts(w0_hl[:, 0], w0_st[:], 1.0)
            tt(w0_hl[:, 1], w0_st[:], w0_hl[:, 0].bitcast(F32), ALU.subtract, "weights")

            def make_A(s, p):
                wait(dve, R_done[s], p)
                dve.tensor_scalar(A_sb[s][:], G_mv[:], col(V_E2, p * 2 + s), None, ALU.mult).then_inc(A_made[s], 1)

            def split_x(s, p):
                wait(dve, xh_made[s], p + 1)
                dve.scalar_tensor_tensor(out=xs[s][:, 1, 0:NXS - 1], in0=xin[s][:, 0:2 * NXS - 2:2],
                                         scalar=col(V_S0, p * 2 + s), in1=xs[s][:, 0, 0:NXS - 1].bitcast(F32),
                                         op0=ALU.mult, op1=ALU.subtract).then_inc(xl_made[s], 1)

            def split_x0(s, p):
                wait(dve, x0_evac[s], p + 1)
                wait(dve, main_done[s], p)
                src = x0f[s][:].rearrange("p a j -> p (a j)")
                dve.tensor_copy(x0[s][:, 0, :], src).then_inc(x0h_made[s], 1)
                dve.wait_ge(x0h_made[s], p + 1)
                dve.tensor_tensor(x0[s][:, 1, :], src, x0[s][:, 0, :].bitcast(F32), ALU.subtract)\
                   .then_inc(x0l_made[s], 1)

            def evac_H(p):
                wait(dve, Hh_made, p + 1)
                dve.tensor_tensor(H_hl[:, 1], p_H[:, 0:NH * C].rearrange("p (a c) -> p a c", c=C),
                                  H_hl[:, 0].bitcast(F32), ALU.subtract).then_inc(Hl_made, 1)
                dve.wait_ge(Hl_made, p + 1)
                wait(dve, main_done[0], p)
                for h in range(2):
                    dve.tensor_copy(H_st[0][h * C:(h + 1) * C, :, h:h + NH, :], H_hl[0:C].bitcast(F32))\
                       .then_inc(H_placed[0], 1)

            def finish(s, p):
                wait(dve, main_done[s], p + 1)
                wait(dve, xr_made[s], p + 1)
                wait(dve, stored[s], 16 * p)
                n = p * 2 + s
                k = NM - 1
                for h, (m0, c0) in enumerate(((1, EDGE + 1), (0, EDGE))):
                    cols = slice(c0, c0 + 2 * k - 1, 2)
                    dve.scalar_tensor_tensor(out=ot[s][:, cols], in0=p_out[s][h * C:(h + 1) * C, m0:m0 + k],
                                             scalar=col(V_D3, n, h * C, (h + 1) * C), in1=xr[s][:, cols],
                                             op0=ALU.mult, op1=ALU.add).then_inc(out_made[s], 1)

            for s in range(2):
                make_A(s, 0)
                split_x(s, 0)
            for s in range(2):
                make_A(s, 1)
            split_x0(0, 0)
            evac_H(0)
            split_x0(1, 0)

            def bc(v, rows, width):
                return vec[rows, v, 0:B].unsqueeze(2).to_broadcast([rows.stop - rows.start, B, width])

            lo, all_ = slice(0, C), slice(0, P)
            dve.wait_ge(e_loaded, 32)
            for side in range(2):
                tt(xse[:, side], xe[:, side], bc(V_S0, lo, 8), ALU.mult, "xse" if side else None)
            ts(yc[:], vec[:, V_SB1, 0:B], 2.0)

            def edge(dst, src, rows, width, scale, offset, name, times=1.0):
                for side in range(2):
                    first = 1 - side
                    d = dst[:, side, :, first:first + width]
                    a = src[rows, side * B * width:(side + 1) * B * width].rearrange("p (b n) -> p b n", n=width)
                    tt(d, a, bc(scale, rows, width), ALU.mult)
                    stt(d, bc(offset, rows, width), times, d, ALU.mult, ALU.add,
                        name if side and name else None)

            dve.wait_ge(put["x0e"], 1)
            edge(x0e, p_out[0], lo, 6, V_A0, V_B0, "x0e")
            dve.wait_ge(put["ye"], 1)
            edge(ye, p_out[1], all_, 5, V_E1, V_SB1, None, 2.0)
            stt(ye[0:C, 0, :, 1], vec[0:C, V_SB1, 0:B], -0.25, ye[0:C, 0, :, 1], ALU.mult, ALU.add)
            stt(ye[C:P, 1, :, 4], vec[C:P, V_SB1, 0:B], -0.25, ye[C:P, 1, :, 4], ALU.mult, ALU.add, "ye")
            dve.wait_ge(put["ze"], 1)
            tt(zc[:], p_out[0][:, 2 * B * 4:2 * B * 4 + B], vec[:, V_E2, 0:B], ALU.mult)
            tt(zc[:], zc[:], vec[:, V_SB2, 0:B], ALU.add)
            edge(ze, p_out[0], all_, 4, V_E2, V_SB2, "ze")
            dve.wait_ge(put["oe"], 1)
            no = 2 * B * EDGE
            tt(vec[0:C, V_C, 0:B], p_out[1][0:C, no:no + B], vec[0:C, V_D3, 0:B], ALU.mult)
            ts(vec[0:C, V_C, 0:B], vec[0:C, V_C, 0:B], bias[0:C, 3:4], op0=ALU.add, name="c")
            for side in range(2):
                a = p_out[1][0:C, side * B * EDGE:(side + 1) * B * EDGE].rearrange("p (b n) -> p b n", n=EDGE)
                d = oe[:, :, side, :]
                tt(d, a, bc(V_D3, lo, EDGE), ALU.mult)
                ts(d, d, bias[0:C, 3:4], op0=ALU.add)
                first = 4 if side else 1
                tt(d, d, xe[:, side, :, first:first + EDGE], ALU.add, "oe" if side else None)

            def turn(p):
                split_x(0, p + 1)
                make_A(0, p + 2)
                finish(0, p)
                split_x(1, p + 1)
                make_A(1, p + 2)
                split_x0(0, p + 1)
                evac_H(p + 1)
                finish(1, p)
                split_x0(1, p + 1)

            turn(0)
            with dve.Fori(1, PAIRS - 1) as p:
                turn(p)
            finish(0, PAIRS - 1)
            finish(1, PAIRS - 1)


_INS = ["x", "cond_512", "L0_cond_weights", "L0_cond_biases", "L0_cond_mod_w", "L0_cond_mod_b"]


def kernel(**inputs):
    import numpy as _np
    import concourse.bacc as _bacc
    from concourse import mybir as _mybir
    from concourse.bass_utils import run_bass_kernel_spmd as _run

    nc = _bacc.Bacc("TRN2", target_bir_lowering=False, num_devices=1)
    arrays, args = {}, []
    for name in _INS:
        a = _np.ascontiguousarray(inputs[name])
        arrays[f"in_{name}_dram"] = a
        args.append(nc.dram_tensor(f"in_{name}_dram", a.shape, _mybir.dt.from_np(a.dtype), kind="ExternalInput").ap())
    shape = inputs["x"].shape
    args.append(nc.dram_tensor("out_0_dram", shape, _mybir.dt.float32, kind="ExternalOutput").ap())
    modulated_conv_kernel(nc, *args)
    r = _run(nc, [arrays], core_ids=[0])
    return r.results[0]["out_0_dram"]
```

```python
from contextlib import ExitStack

import concourse.bass as bass
from concourse import mybir

F32 = mybir.dt.float32
F32R = mybir.dt.float32r
ACT = mybir.ActivationFunctionType
ALU = mybir.AluOpType
AX_X = mybir.AxisListType.X

P = 128
PASSES = ((0, 0), (0, 1), (1, 0))
V_S0, V_A0, V_B0, V_E1, V_E2, V_D3, V_C, V_SB1, V_SB2, NVEC = range(10)


def modulated_conv_kernel(nc, x, cond, weights, biases, mod_w, mod_b, out):
    B, C, L = x.shape
    LAYERS, _, _, K = weights.shape
    STYLE = cond.shape[1]
    PAIRS = B // 2
    HALF = L // 2
    SCALE2 = 1.0 / (C * K * K)
    SCALE = float(SCALE2 ** 0.5)
    EPS = 1e-8
    BP = B + 2
    XW = L + 12
    NXS = HALF + 6
    NJ = (HALF + 4) // 2
    NM = HALF - 2
    NR, NA, NH = 5, 4, 7
    EDGE = 3

    ctx = ExitStack()
    with ctx:
        def sb(name, shape, dt=F32):
            return ctx.enter_context(nc.sbuf_tensor(name, shape, dt))

        def ps(name, shape):
            return ctx.enter_context(nc.psum_tensor(name, shape, F32))

        def sem(name):
            return ctx.enter_context(nc.semaphore(name))

        def per_slot(make, name, *a):
            return [make(f"{name}{s}", *a) for s in range(2)]

        ident = sb("ident", [P, P])
        wn = sb("wn", [C, LAYERS, C, K])
        mwn = sb("mwn", [P, 2, STYLE])
        cn = sb("cn", [B, STYLE])
        bn = sb("bn", [LAYERS, 2, C])
        biases2 = sb("biases2", [P, 2, LAYERS])
        mbias, bias = biases2[:, 0], biases2[:, 1]
        mwT = sb("mwT", [P, LAYERS, 2, C])
        cT = sb("cT", [P, B])
        style = sb("style", [P, LAYERS, B])
        style2 = sb("style2", [P, LAYERS, B])
        wsq = sb("wsq", [C, LAYERS, C, K])
        wsum = sb("wsum", [C, LAYERS, C])
        wsumT = sb("wsumT", [C, LAYERS, 2, C])
        dt_ = sb("dt_", [P, LAYERS, B])
        dq = sb("dq", [P, LAYERS, B])
        dr = sb("dr", [P, LAYERS, B])
        da = sb("da", [P, LAYERS, B])
        dm = sb("dm", [P, LAYERS, B])
        vec = sb("vec", [P, NVEC, BP])
        blur = sb("blur", [C, 2, 8, C])
        F_st = sb("F_st", [P, 3, C])
        V_st = sb("V_st", [P, 2, P])
        V_hl = sb("V_hl", [P, 2, 2, P], F32R)
        G_mv = sb("G_mv", [P, NA, C])
        w0T = sb("w0T", [P, K, C])
        w0_st = sb("w0_st", [P, 2, P])
        w0_hl = sb("w0_hl", [P, 2, 2, P], F32R)
        y_st = sb("y_st", [C, 6, C])
        z_st = sb("z_st", [P, 3, P])
        o_st = sb("o_st", [P, 3, C])
        xe = sb("xe", [C, 2, B, 8])
        xse = sb("xse", [C, 2, B, 8])
        x0e = sb("x0e", [C, 2, B, 7])
        ye = sb("ye", [P, 2, B, 6])
        ze = sb("ze", [P, 2, B, 5])
        yc = sb("yc", [P, B])
        zc = sb("zc", [P, B])
        oe = sb("oe", [C, B, 2, EDGE])
        xin = [per_slot(sb, f"xin{par}_", [P, XW]) for par in range(2)]
        xs = per_slot(sb, "xs", [P, 2, NXS], F32R)
        xr = [per_slot(sb, f"xr{par}_", [C, L]) for par in range(2)]
        x0f = per_slot(sb, "x0f", [P, 2, NJ])
        x0 = per_slot(sb, "x0", [P, 2, 2 * NJ], F32R)
        A_sb = per_slot(sb, "A_sb", [P, 2, NA, C], F32R)
        R_sb = per_slot(sb, "R_sb", [P, NR, C])
        H_hl = sb("H_hl", [P, 2, NH, C], F32R)
        H_st = per_slot(sb, "H_st", [P, 2, NH + 1, C], F32R)
        ot = per_slot(sb, "ot", [C, L])
        p_l0 = per_slot(ps, "p_l0", [P, 2, 512])
        p_out = per_slot(ps, "p_out", [P, 512])
        p_R = ps("p_R", [P, 512])
        p_H = ps("p_H", [P, 512])

        zeroed = sem("zeroed")
        ident_made = sem("ident_made")
        w_loaded = sem("w_loaded")
        mw_loaded = sem("mw_loaded")
        cond_loaded = sem("cond_loaded")
        b_loaded = sem("b_loaded")
        e_loaded = sem("e_loaded")
        x_loaded = [per_slot(sem, f"x_loaded{par}_") for par in range(2)]
        put = {n: sem(f"put_{n}") for n in ("styleT", "w0T", "w2T", "wsumT", "style", "demod", "GT", "FT",
                                            "x0e", "ye", "ze", "oe", "zc", "oc")}
        copied = {n: sem(f"copied_{n}") for n in ("styleT", "w0_st", "w0h", "G_mv", "F_st", "rest")}
        made = {n: sem(f"made_{n}") for n in ("wsum", "wsumT", "style2", "blur", "dt", "s0", "vec", "V", "w0l", "y_st",
                                              "zc", "xse", "x0e", "ye", "ze", "yc", "c", "oe")}
        dve_step = sem("dve_step")
        act_step = sem("act_step")
        sqrt_done = sem("sqrt_done")
        xh_made = per_slot(sem, "xh_made")
        xl_made = per_slot(sem, "xl_made")
        xr_made = per_slot(sem, "xr_made")
        l0_done = per_slot(sem, "l0_done")
        x0_evac = per_slot(sem, "x0_evac")
        x0h_made = per_slot(sem, "x0h_made")
        x0l_made = per_slot(sem, "x0l_made")
        Ah_made = per_slot(sem, "Ah_made")
        Al_made = per_slot(sem, "Al_made")
        R_done = per_slot(sem, "R_done")
        R_evac = per_slot(sem, "R_evac")
        H_done = sem("H_done")
        Hh_made = sem("Hh_made")
        Hl_made = sem("Hl_made")
        H_placed = per_slot(sem, "H_placed")
        main_done = per_slot(sem, "main_done")
        out_made = per_slot(sem, "out_made")
        edge_put = per_slot(sem, "edge_put")
        stored = per_slot(sem, "stored")

        def wait(eng, s, value):
            if not isinstance(value, int) or value > 0:
                eng.wait_ge(s, value)

        def col(v, n, lo=0, hi=P):
            return vec[lo:hi, v, bass.ds(n, 1)]

        block = ctx.enter_context(nc.Block())

        @block.gpsimd
        def _(pool):
            for par in range(2):
                for s in range(2):
                    pool.memset(xin[par][s][:, 0:2], 0.0).then_inc(zeroed, 1)
                    pool.memset(xin[par][s][:, L:XW], 0.0).then_inc(zeroed, 1)
            pool.memset(ident[:], 0.0).then_inc(zeroed, 1)
            pool.wait_ge(zeroed, 9)
            pool.affine_select(out=ident[:], in_=ident[:], compare_op=ALU.not_equal, fill=1.0, base=0,
                               pattern=[[-1, P]], channel_multiplier=1).then_inc(ident_made, 1)
            for t in (w0_st, V_st, vec, blur, xe, z_st, x0e, ye, ze):
                pool.memset(t[:], 0.0).then_inc(zeroed, 1)
            count = 18
            for s in range(2):
                for rows, block in ((slice(0, C), NH), (slice(C, P), 0)):
                    pool.wait_ge(zeroed, count)
                    pool.memset(H_st[s][rows, :, block, :].bitcast(F32), 0.0).then_inc(zeroed, 1)
                    count += 1
            pool.wait_ge(zeroed, count)
            pool.wait_ge(made["oe"], 1)
            def put_edges(p):
                for s in range(2):
                    wait(pool, stored[s], 16 * p)
                    n = p * 2 + s
                    pool.tensor_copy(ot[s][:, 0:EDGE], oe[:, bass.ds(n, 1), 0, :].rearrange("c a n -> c (a n)"))\
                        .then_inc(edge_put[s], 1)
                    pool.tensor_copy(ot[s][:, L - EDGE:L], oe[:, bass.ds(n, 1), 1, :].rearrange("c a n -> c (a n)"))\
                        .then_inc(edge_put[s], 1)

            put_edges(0)
            with pool.Fori(1, PAIRS) as p:
                put_edges(p)

        @block.sync
        def _(sp):
            sp.dma_start(wn[:], weights.rearrange("l o i k -> o l i k")).then_inc(w_loaded, 16)
            sp.dma_start(mwn[:], mod_w.rearrange("(t l) c s -> (l c) t s", t=2)).then_inc(mw_loaded, 16)
            sp.dma_start(cn[:], cond).then_inc(cond_loaded, 16)

            def load(s, p, par):
                n = p * 2 + s
                wait(sp, xl_made[s], p - 1)
                wait(sp, xr_made[s], p - 1)
                src = x[bass.ds(n, 1), :, :].rearrange("a c l -> (a c) l")
                sp.dma_start(xin[par][s][0:C, 2:2 + L], src).then_inc(x_loaded[par][s], 16)
                sp.dma_start(xin[par][s][C:P, 1:1 + L], src).then_inc(x_loaded[par][s], 16)

            def place_H(p):
                wait(sp, Hl_made, p + 1)
                wait(sp, main_done[1], p)
                sp.dma_start(H_st[1][0:C, :, 0:NH, :].bitcast(F32), H_hl[C:P].bitcast(F32)).then_inc(H_placed[1], 16)
                sp.dma_start(H_st[1][C:P, :, 1:NH + 1, :].bitcast(F32), H_hl[C:P].bitcast(F32)).then_inc(H_placed[1], 16)

            def store(s, p):
                n = p * 2 + s
                wait(sp, out_made[s], 2 * (p + 1))
                wait(sp, edge_put[s], 2 * (p + 1))
                dst = out[bass.ds(n, 1), :, :].rearrange("a c l -> (a c) l")
                sp.dma_start(dst, ot[s][:]).then_inc(stored[s], 16)

            sp.wait_ge(zeroed, 8)
            load(0, 0, 0)
            sp.dma_start(bn[:, 0, :], mod_b).then_inc(b_loaded, 16)
            sp.dma_start(bn[:, 1, :], biases).then_inc(b_loaded, 16)
            load(1, 0, 0)
            load(0, 1, 1)
            load(1, 1, 1)
            sp.wait_ge(zeroed, 14)
            sp.dma_start(xe[:, 0, :, 1:8], x[:, :, 0:7].rearrange("b c n -> c b n")).then_inc(e_loaded, 16)
            sp.dma_start(xe[:, 1, :, 0:7], x[:, :, L - 7:L].rearrange("b c n -> c b n")).then_inc(e_loaded, 16)
            place_H(0)

            def turn(p, par):
                load(0, p + 2, par)
                store(0, p)
                load(1, p + 2, par)
                place_H(p + 1)
                store(1, p)

            turn(0, 0)
            turn(1, 1)
            with sp.Fori(1, PAIRS // 2 - 1) as i:
                turn(i * 2, 0)
                turn(i * 2 + 1, 1)
            p = PAIRS - 2
            store(0, p)
            place_H(p + 1)
            store(1, p)
            for s in range(2):
                store(s, PAIRS - 1)
            for s in range(2):
                sp.wait_ge(stored[s], 16 * PAIRS)

        @block.tensor
        def _(pe):
            pe.wait_ge(ident_made, 1)
            pe.wait_ge(w_loaded, 16)

            def transpose_taps(bank, l):
                for k in range(K):
                    for h in range(2):
                        ins = pe.matmul(bank[h * C:(h + 1) * C, k * C:(k + 1) * C], wn[:, l, :, k],
                                        ident[0:C, 0:C], start=True, stop=True)
                return ins

            transpose_taps(p_out[0], 0).then_inc(put["w0T"], 1)
            pe.wait_ge(mw_loaded, 16)
            pe.wait_ge(cond_loaded, 16)
            for t in range(2):
                pe.transpose(p_l0[0][:, 0, t * P:(t + 1) * P], mwn[:, t, :], ident[:])
            pe.transpose(p_l0[0][:, 0, 2 * P:2 * P + B], cn[:], ident[0:B, 0:B]).then_inc(put["styleT"], 1)
            pe.wait_ge(made["wsum"], 1)
            for l in range(LAYERS):
                ins = pe.transpose(p_l0[1][0:C, 0, l * C:(l + 1) * C], wsum[:, l, :], ident[0:C, 0:C])
            ins.then_inc(put["wsumT"], 1)
            pe.wait_ge(b_loaded, 32)
            for j in range(2):
                b0 = LAYERS * B + j * LAYERS
                for h in range(2):
                    pe.matmul(p_l0[0][h * C:(h + 1) * C, 1, b0:b0 + LAYERS], bn[:, j, :], ident[0:LAYERS, 0:LAYERS],
                              start=True, stop=True)
            pe.wait_ge(copied["styleT"], 1)
            for l in range(LAYERS):
                ins = pe.matmul(p_l0[0][:, 1, l * B:(l + 1) * B], mwT[:, l].rearrange("p a c -> p (a c)"), cT[:],
                                start=True, stop=True)
            ins.then_inc(put["style"], 1)
            pe.wait_ge(made["blur"], 1)
            for m in range(NA):
                k0 = (NA - 1 - m) * C
                pe.transpose(p_out[1][:, k0:k0 + C], blur[:, 1, 2 * m:2 * m + 2, :].rearrange("p t i -> p (t i)"),
                             ident[0:C, 0:C])
            for m in range(3):
                k0 = (NA + m) * C
                ins = pe.transpose(p_out[1][:, k0:k0 + C],
                                   blur[:, 1, 2 * m + 1:2 * m + 3, :].rearrange("p t i -> p (t i)"),
                                   ident[0:C, 0:C])
            ins.then_inc(put["GT"], 1)
            pe.wait_ge(made["wsumT"], 1)
            pe.wait_ge(made["style2"], 1)
            for l in range(LAYERS):
                ins = pe.matmul(p_l0[1][:, 1, l * B:(l + 1) * B], wsumT[:, l].rearrange("p a c -> p (a c)"),
                                style2[0:C, l, :], start=True, stop=True)
            ins.then_inc(put["demod"], 1)
            for m in range(3):
                ins = pe.transpose(p_R[:, m * C:(m + 1) * C],
                                   blur[:, 0, 2 * m + 1:2 * m + 3, :].rearrange("p t i -> p (t i)"),
                                   ident[0:C, 0:C])
            ins.then_inc(put["FT"], 1)
            transpose_taps(p_H, 2).then_inc(put["w2T"], 1)

            def compose_R(s, p):
                wait(pe, Al_made[s], p + 1)
                if s == 0:
                    wait(pe, R_evac[1], p)
                else:
                    wait(pe, R_evac[0], p + 1)
                for q, (a, b) in enumerate(PASSES):
                    for st in range(2):
                        ins = pe.matmul(p_R[:, st * C:(st + NA) * C], V_hl[:, a, st, :],
                                        A_sb[s][:, b].rearrange("p a c -> p (a c)"),
                                        start=(q == 0 and st == 0), stop=(q == 2 and st == 1),
                                        skip_group_check=True)
                ins.then_inc(R_done[s], 1)

            def compose_H(p):
                wait(pe, Hl_made, p)
                wait(pe, R_evac[0], p + 1)
                wait(pe, R_evac[1], p + 1)
                for c in range(3):
                    for s in range(2):
                        ins = pe.matmul(p_H[s * C:(s + 1) * C, c * C:(c + NR) * C], F_st[:, c, :],
                                        R_sb[s][:].rearrange("p a c -> p (a c)"), start=(c == 0), stop=(c == 2),
                                        skip_group_check=True)
                ins.then_inc(H_done, 1)

            def layer0(s, p):
                wait(pe, xl_made[s], p + 1)
                wait(pe, x0_evac[s], p)
                for bank in range(2):
                    for q, (a, b) in enumerate(PASSES):
                        for st in range(2):
                            e0 = bank * NJ + st
                            ins = pe.matmul(p_l0[s][:, bank, 0:NJ], w0_hl[:, a, st, :], xs[s][:, b, e0:e0 + NJ],
                                            start=(q == 0 and st == 0), stop=(q == 2 and st == 1))
                ins.then_inc(l0_done[s], 1)

            def main(s, p):
                if s == 0:
                    wait(pe, H_placed[0], 2 * (p + 1))
                else:
                    wait(pe, H_placed[1], 32 * (p + 1))
                wait(pe, x0l_made[s], p + 1)
                wait(pe, out_made[s], 2 * p)
                for q, (a, b) in enumerate(PASSES):
                    for t in range(4):
                        blk = NH - 1 - 2 * t
                        ins = pe.matmul(p_out[s][:, 0:NM],
                                        H_st[s][:, a, blk:blk + 2, :].rearrange("p a c -> p (a c)"),
                                        x0[s][:, b, t:t + NM], start=(q == 0 and t == 0), stop=(q == 2 and t == 3))
                ins.then_inc(main_done[s], 1)

            pe.wait_ge(made["w0l"], 1)
            pe.wait_ge(made["style2"], 1)
            pe.wait_ge(copied["styleT"], 1)
            layer0(0, 0)
            pe.wait_ge(made["V"], 1)
            pe.wait_ge(copied["F_st"], 1)
            compose_R(0, 0)
            pe.wait_ge(made["dt"], 1)
            layer0(1, 0)
            compose_R(1, 0)
            pe.wait_ge(copied["rest"], 1)
            pe.wait_ge(made["yc"], 1)
            for k in range(3):
                ins = pe.matmul(p_out[1][:, 0:B], z_st[:, k, :], yc[:], start=(k == 0), stop=(k == 2))
            ins.then_inc(put["zc"], 1)
            compose_H(0)
            pe.wait_ge(made["zc"], 1)
            for k in range(3):
                ins = pe.matmul(p_out[1][0:C, 0:B], o_st[:, k, :], zc[:], start=(k == 0), stop=(k == 2))
            ins.then_inc(put["oc"], 1)

            pe.wait_ge(zeroed, 22)

            p_e = p_l0[1][:, 0]

            def edge_x0():
                pe.wait_ge(made["xse"], 1)
                pe.wait_ge(x0_evac[1], 1)
                for k in range(K):
                    ins = pe.matmul(p_e[0:C, 0:2 * B * 6], w0T[0:C, k, :], xse[:, :, :, k:k + 6],
                                    start=(k == 0), stop=(k == K - 1))
                ins.then_inc(put["x0e"], 1)

            def edge_y():
                pe.wait_ge(made["x0e"], 1)
                for k in range(K):
                    c = 4 - 2 * k
                    ins = pe.matmul(p_e[:, 0:2 * B * 5], y_st[:, c:c + 2, :].rearrange("p a c -> p (a c)"),
                                    x0e[:, :, :, k:k + 5], start=(k == 0), stop=(k == K - 1))
                ins.then_inc(put["ye"], 1)

            def edge_z():
                pe.wait_ge(made["ye"], 1)
                for k in range(3):
                    ins = pe.matmul(p_e[:, 0:2 * B * 4], z_st[:, k, :], ye[:, :, :, k:k + 4],
                                    start=(k == 0), stop=(k == 2))
                ins.then_inc(put["ze"], 1)

            def edge_out():
                pe.wait_ge(made["ze"], 1)
                for k in range(3):
                    ins = pe.matmul(p_e[0:C, 0:2 * B * EDGE], o_st[:, k, :], ze[:, :, :, k:k + EDGE],
                                    start=(k == 0), stop=(k == 2))
                ins.then_inc(put["oe"], 1)

            def turn(p):
                compose_R(0, p + 1)
                main(0, p)
                compose_R(1, p + 1)
                layer0(0, p + 1)
                compose_H(p + 1)
                main(1, p)
                layer0(1, p + 1)

            compose_R(0, 1)
            edge_x0()
            main(0, 0)
            edge_y()
            compose_R(1, 1)
            layer0(0, 1)
            edge_z()
            compose_H(1)
            pe.wait_ge(made["c"], 1)
            main(1, 0)
            edge_out()
            pe.wait_ge(made["oe"], 1)
            layer0(1, 1)
            with pe.Fori(1, PAIRS - 1) as p:
                turn(p)
            main(0, PAIRS - 1)
            main(1, PAIRS - 1)

        @block.scalar
        def _(act):
            def copy(o, a, signal=act_step):
                act.activation(o, a, ACT.Copy).then_inc(signal, 1)

            act.wait_ge(zeroed, 10)
            act.wait_ge(put["w0T"], 1)
            wT = p_out[0][:, 0:3 * C].rearrange("p (k c) -> p k c", c=C)
            copy(w0_st[0:C, 0, 0:C], wT[0:C, 0])
            copy(w0_st[C:P, 0, 0:C], wT[C:P, 1])
            copy(w0_st[C:P, 0, C:P], wT[C:P, 0])
            copy(w0_st[0:C, 1, 0:C], wT[0:C, 2])
            copy(w0_st[0:C, 1, C:P], wT[0:C, 1])
            copy(w0_st[C:P, 1, C:P], wT[C:P, 2], copied["w0_st"])
            act.wait_ge(put["styleT"], 1)
            copy(cT[:], p_l0[0][:, 0, 2 * P:2 * P + B])
            for h in range(2):
                copy(mwT[:, :, h, :], p_l0[0][:, 0, 0:2 * P].rearrange("p (l c) -> p l c", c=C),
                     copied["styleT"] if h else act_step)
            act.wait_ge(copied["w0_st"], 1)
            copy(w0_hl[:, 0], w0_st[:], copied["w0h"])
            act.wait_ge(put["GT"], 1)
            act.activation(G_mv[:], p_out[1][:, 0:NA * C].rearrange("p (a c) -> p a c", c=C), ACT.Copy,
                           scale=0.125).then_inc(copied["G_mv"], 1)

            def split_x(s, p, par, use):
                wait(act, x_loaded[par][s], 32 * (use + 1))
                wait(act, l0_done[s], p)
                act.activation(xs[s][:, 0, 0:NXS - 1], xin[par][s][:, 0:2 * NXS - 2:2], ACT.Copy,
                               scale=col(V_S0, p * 2 + s)).then_inc(xh_made[s], 1)

            def make_A(s, p):
                wait(act, R_done[s], p)
                act.activation(A_sb[s][:, 0], G_mv[:], ACT.Copy, scale=col(V_E2, p * 2 + s)).then_inc(Ah_made[s], 1)

            def evac_R(s, p):
                wait(act, R_done[s], p + 1)
                wait(act, H_done, p)
                act.activation(R_sb[s][:].rearrange("p a c -> p (a c)"), p_R[:, 0:NR * C], ACT.Copy,
                               scale=col(V_E1, p * 2 + s)).then_inc(R_evac[s], 1)

            def evac_x0(s, p):
                wait(act, l0_done[s], p + 1)
                wait(act, x0l_made[s], p)
                n = p * 2 + s
                act.activation(x0f[s][:], p_l0[s][:, :, 0:NJ], ACT.Identity, scale=col(V_A0, n),
                               bias=col(V_B0, n)).then_inc(x0_evac[s], 1)

            def evac_H(p):
                wait(act, H_done, p + 1)
                wait(act, H_placed[0], 2 * p)
                wait(act, H_placed[1], 32 * p)
                act.activation(H_hl[:, 0], p_H[:, 0:NH * C].rearrange("p (a c) -> p a c", c=C), ACT.Copy)\
                   .then_inc(Hh_made, 1)

            def residual(s, p, par):
                wait(act, out_made[s], 2 * (p - 1))
                act.activation(xr[par][s][:], xin[par][s][0:C, 2:2 + L], ACT.Identity, bias=col(V_C, p * 2 + s, 0, C))\
                   .then_inc(xr_made[s], 1)

            act.wait_ge(made["s0"], 1)
            split_x(0, 0, 0, 0)
            act.wait_ge(made["dt"], 1)
            act.activation(dq[:], dt_[:], ACT.Sqrt).then_inc(sqrt_done, 1)
            split_x(1, 0, 0, 0)
            act.wait_ge(put["FT"], 1)
            act.activation(F_st[:], p_R[:, 0:3 * C].rearrange("p (a c) -> p a c", c=C), ACT.Copy,
                           scale=0.25).then_inc(copied["F_st"], 1)
            act.wait_ge(made["vec"], 1)
            act.wait_ge(copied["G_mv"], 1)
            make_A(0, 0)
            make_A(1, 0)
            evac_x0(0, 0)
            evac_R(0, 0)
            make_A(0, 1)
            evac_R(1, 0)
            make_A(1, 1)
            act.wait_ge(zeroed, 15)
            act.wait_ge(put["w2T"], 1)
            act.activation(o_st[:], p_out[1][:, NA * C:(NA + 3) * C].rearrange("p (a c) -> p a c", c=C), ACT.Copy,
                           scale=0.125).then_inc(act_step, 1)
            copy(w0T[:], wT)
            w2T = p_H[:, 0:3 * C].rearrange("p (k c) -> p k c", c=C)
            copy(z_st[C:P, 0, 0:C], w2T[C:P, 0])
            copy(z_st[0:C, 1, 0:C], w2T[0:C, 1])
            copy(z_st[0:C, 1, C:P], w2T[0:C, 0])
            copy(z_st[C:P, 1, 0:C], w2T[C:P, 2])
            copy(z_st[C:P, 1, C:P], w2T[C:P, 1])
            copy(z_st[0:C, 2, C:P], w2T[0:C, 2], copied["rest"])
            evac_x0(1, 0)
            evac_H(0)
            act.wait_ge(made["c"], 1)
            residual(0, 0, 0)
            residual(1, 0, 0)

            def turn(p, par, use):
                split_x(0, p + 1, 1 - par, use)
                evac_R(0, p + 1)
                make_A(0, p + 2)
                split_x(1, p + 1, 1 - par, use)
                residual(0, p + 1, 1 - par)
                evac_R(1, p + 1)
                make_A(1, p + 2)
                residual(1, p + 1, 1 - par)
                evac_x0(0, p + 1)
                evac_H(p + 1)
                evac_x0(1, p + 1)

            turn(0, 0, 0)
            with act.Fori(0, PAIRS // 2 - 1) as i:
                turn(i * 2 + 1, 1, i + 1)
                turn(i * 2 + 2, 0, i + 1)

        @block.vector
        def _(dve):
            n_step = [0]

            def step(ins, name=None):
                if name:
                    ins.then_inc(made[name], 1)
                    last[0] = (made[name], 1)
                else:
                    n_step[0] += 1
                    ins.then_inc(dve_step, 1)
                    last[0] = (dve_step, n_step[0])

            last = [None]

            def then():
                dve.wait_ge(*last[0])

            def tt(o, a, b, op, name=None):
                step(dve.tensor_tensor(o, a, b, op), name)

            def ts(o, a, s1, s2=None, op0=ALU.mult, op1=ALU.bypass, name=None):
                if s2 is None:
                    step(dve.tensor_scalar(o, a, s1, None, op0), name)
                else:
                    step(dve.tensor_scalar(o, a, s1, s2, op0, op1), name)

            def stt(o, a, s1, b, op0, op1, name=None):
                step(dve.scalar_tensor_tensor(out=o, in0=a, scalar=s1, in1=b, op0=op0, op1=op1), name)

            dve.wait_ge(w_loaded, 16)
            tt(wsq[:], wn[:], wn[:], ALU.mult)
            then()
            step(dve.tensor_reduce(wsum[:], wsq[:], AX_X, ALU.add), "wsum")
            dve.wait_ge(zeroed, 13)
            w = [wn[:, 1:4:2, :, k] for k in range(K)]
            u = [blur[:, :, c + 1, :] for c in range(6)]
            stt(u[1], w[0], 3.0, w[1], ALU.mult, ALU.add)
            stt(u[4], w[2], 3.0, w[1], ALU.mult, ALU.add)
            ts(u[0], w[0], 1.0)
            ts(u[5], w[2], 1.0)
            then()
            stt(u[2], w[1], 2.0, u[1], ALU.mult, ALU.add)
            stt(u[3], w[1], 2.0, u[4], ALU.mult, ALU.add)
            then()
            tt(u[2], u[2], w[2], ALU.add)
            tt(u[3], u[3], w[0], ALU.add, "blur")
            dve.wait_ge(put["wsumT"], 1)
            for h in range(2):
                ts(wsumT[:, :, h, :], p_l0[1][0:C, 0, 0:LAYERS * C].rearrange("p (l c) -> p l c", c=C), 1.0,
                   name="wsumT" if h else None)
            dve.wait_ge(put["style"], 1)
            ts(biases2[:].rearrange("p j l -> p (j l)"), p_l0[0][:, 1, LAYERS * B:LAYERS * (B + 2)], 1.0)
            then()
            tt(style[:], p_l0[0][:, 1, 0:LAYERS * B].rearrange("p (l b) -> p l b", b=B),
               mbias.unsqueeze(2).to_broadcast([P, LAYERS, B]), ALU.add)
            then()
            tt(style2[:], style[:], style[:], ALU.mult, "style2")
            dve.wait_ge(zeroed, 12)
            ts(vec[:, V_S0, 0:B], style[:, 0, :], 1.0, name="s0")
            ts(vec[:, V_B0, 0:B], style[:, 1, :], 1.0)
            tt(vec[:, V_E1, 0:B], style[:, 2, :], style[:, 1, :], ALU.mult)
            ts(vec[:, V_SB1, 0:B], style[:, 2, :], bias[:, 1:2])
            ts(vec[:, V_SB2, 0:B], style[:, 3, :], bias[:, 2:3])
            dve.wait_ge(put["demod"], 1)
            ts(dt_[:], p_l0[1][:, 1, 0:LAYERS * B].rearrange("p (l b) -> p l b", b=B), SCALE2, EPS,
               ALU.mult, ALU.add, "dt")
            dve.wait_ge(copied["w0h"], 1)
            tt(w0_hl[:, 1], w0_st[:], w0_hl[:, 0].bitcast(F32), ALU.subtract, "w0l")
            dve.wait_ge(sqrt_done, 1)
            step(dve.reciprocal(dr[:], dq[:]))

            def make_A(s, p):
                wait(dve, Ah_made[s], p + 1)
                dve.scalar_tensor_tensor(out=A_sb[s][:, 1], in0=G_mv[:], scalar=col(V_E2, p * 2 + s),
                                         in1=A_sb[s][:, 0].bitcast(F32), op0=ALU.mult, op1=ALU.subtract)\
                    .then_inc(Al_made[s], 1)

            def split_x(s, p, par):
                wait(dve, xh_made[s], p + 1)
                dve.scalar_tensor_tensor(out=xs[s][:, 1, 0:NXS - 1], in0=xin[par][s][:, 0:2 * NXS - 2:2],
                                         scalar=col(V_S0, p * 2 + s), in1=xs[s][:, 0, 0:NXS - 1].bitcast(F32),
                                         op0=ALU.mult, op1=ALU.subtract).then_inc(xl_made[s], 1)

            def split_x0(s, p):
                wait(dve, x0_evac[s], p + 1)
                wait(dve, main_done[s], p)
                src = x0f[s][:].rearrange("p a j -> p (a j)")
                dve.tensor_copy(x0[s][:, 0, :], src).then_inc(x0h_made[s], 1)
                dve.wait_ge(x0h_made[s], p + 1)
                dve.tensor_tensor(x0[s][:, 1, :], src, x0[s][:, 0, :].bitcast(F32), ALU.subtract)\
                    .then_inc(x0l_made[s], 1)

            def evac_H(p):
                wait(dve, Hh_made, p + 1)
                dve.tensor_tensor(H_hl[:, 1], p_H[:, 0:NH * C].rearrange("p (a c) -> p a c", c=C),
                                  H_hl[:, 0].bitcast(F32), ALU.subtract).then_inc(Hl_made, 1)
                dve.wait_ge(Hl_made, p + 1)
                wait(dve, main_done[0], p)
                for h in range(2):
                    dve.tensor_copy(H_st[0][h * C:(h + 1) * C, :, h:h + NH, :], H_hl[0:C].bitcast(F32))\
                       .then_inc(H_placed[0], 1)

            def finish(s, p, par):
                wait(dve, main_done[s], p + 1)
                wait(dve, xr_made[s], p + 1)
                wait(dve, stored[s], 16 * p)
                n = p * 2 + s
                k = NM - 1
                for h, (m0, c0) in enumerate(((1, EDGE + 1), (0, EDGE))):
                    cols = slice(c0, c0 + 2 * k - 1, 2)
                    dve.scalar_tensor_tensor(out=ot[s][:, cols], in0=p_out[s][h * C:(h + 1) * C, m0:m0 + k],
                                             scalar=col(V_D3, n, h * C, (h + 1) * C), in1=xr[par][s][:, cols],
                                             op0=ALU.mult, op1=ALU.add).then_inc(out_made[s], 1)

            split_x(0, 0, 0)
            then()
            tt(da[:], dr[:], dr[:], ALU.mult)
            then()
            tt(da[:], da[:], dt_[:], ALU.mult)
            then()
            ts(da[:], da[:], -0.5 * SCALE, 1.5 * SCALE, ALU.mult, ALU.add)
            then()
            tt(dm[:], dr[:], da[:], ALU.mult)
            then()
            tt(vec[:, V_E2, 0:B], style[:, 3, :], dm[:, 2, :], ALU.mult)
            tt(vec[:, V_A0, 0:B], dm[:, 1, :], dm[:, 0, :], ALU.mult)
            ts(vec[:, V_B0, 0:B], dm[:, 1, :], bias[:, 0:1])
            ts(vec[:, V_D3, 0:B], dm[:, 3, :], 1.0, name="vec")
            V = [wn[:, 2, :, K - 1 - b] for b in range(K)]
            ts(V_st[0:C, 0, 0:C], V[0], 1.0)
            ts(V_st[C:P, 0, 0:C], V[1], 1.0)
            ts(V_st[C:P, 0, C:P], V[0], 1.0)
            ts(V_st[0:C, 1, 0:C], V[2], 1.0)
            ts(V_st[0:C, 1, C:P], V[1], 1.0)
            ts(V_st[C:P, 1, C:P], V[2], 1.0)
            then()
            ts(V_hl[:, 0], V_st[:], 1.0)
            then()
            tt(V_hl[:, 1], V_st[:], V_hl[:, 0].bitcast(F32), ALU.subtract, "V")
            make_A(0, 0)
            split_x(1, 0, 0)
            make_A(1, 0)
            ts(yc[:], vec[:, V_SB1, 0:B], 2.0, name="yc")
            ts(y_st[:], blur[:, 0, 1:7, :], 0.25, name="y_st")
            split_x0(0, 0)
            make_A(0, 1)
            make_A(1, 1)

            def bc(v, rows, width):
                return vec[rows, v, 0:B].unsqueeze(2).to_broadcast([rows.stop - rows.start, B, width])

            lo, all_ = slice(0, C), slice(0, P)
            dve.wait_ge(put["zc"], 1)
            tt(zc[:], p_out[1][:, 0:B], vec[:, V_E2, 0:B], ALU.mult)
            then()
            tt(zc[:], zc[:], vec[:, V_SB2, 0:B], ALU.add, "zc")
            split_x0(1, 0)
            evac_H(0)
            dve.wait_ge(put["oc"], 1)
            tt(vec[0:C, V_C, 0:B], p_out[1][0:C, 0:B], vec[0:C, V_D3, 0:B], ALU.mult)
            then()
            ts(vec[0:C, V_C, 0:B], vec[0:C, V_C, 0:B], bias[0:C, 3:4], op0=ALU.add, name="c")
            dve.wait_ge(zeroed, 18)
            dve.wait_ge(e_loaded, 32)
            for side in range(2):
                tt(xse[:, side], xe[:, side], bc(V_S0, lo, 8), ALU.mult, "xse" if side else None)

            def edge(dst, src, rows, width, scale, offset, name, times=1.0):
                d = [dst[:, side, :, 1 - side:1 - side + width] for side in range(2)]
                for side in range(2):
                    a = src[rows, side * B * width:(side + 1) * B * width].rearrange("p (b n) -> p b n", n=width)
                    tt(d[side], a, bc(scale, rows, width), ALU.mult)
                then()
                for side in range(2):
                    stt(d[side], bc(offset, rows, width), times, d[side], ALU.mult, ALU.add,
                        name if side and name else None)

            p_e = p_l0[1][:, 0]

            def edge_x0():
                dve.wait_ge(put["x0e"], 1)
                edge(x0e, p_e, lo, 6, V_A0, V_B0, "x0e")

            def edge_y():
                dve.wait_ge(put["ye"], 1)
                edge(ye, p_e, all_, 5, V_E1, V_SB1, None, 2.0)
                then()
                stt(ye[0:C, 0, :, 1], vec[0:C, V_SB1, 0:B], -0.25, ye[0:C, 0, :, 1], ALU.mult, ALU.add)
                stt(ye[C:P, 1, :, 4], vec[C:P, V_SB1, 0:B], -0.25, ye[C:P, 1, :, 4], ALU.mult, ALU.add, "ye")

            def edge_z():
                dve.wait_ge(put["ze"], 1)
                edge(ze, p_e, all_, 4, V_E2, V_SB2, "ze")

            def edge_out():
                dve.wait_ge(put["oe"], 1)
                for op in range(3):
                    for side in range(2):
                        d = oe[:, :, side, :]
                        if op == 0:
                            a = p_e[0:C, side * B * EDGE:(side + 1) * B * EDGE]
                            tt(d, a.rearrange("p (b n) -> p b n", n=EDGE), bc(V_D3, lo, EDGE), ALU.mult)
                        elif op == 1:
                            ts(d, d, bias[0:C, 3:4], op0=ALU.add)
                        else:
                            first = 4 if side else 1
                            tt(d, d, xe[:, side, :, first:first + EDGE], ALU.add, "oe" if side else None)
                    if op < 2:
                        then()

            def turn(p, par):
                split_x(0, p + 1, 1 - par)
                make_A(0, p + 2)
                split_x(1, p + 1, 1 - par)
                finish(0, p, par)
                make_A(1, p + 2)
                split_x0(0, p + 1)
                evac_H(p + 1)
                finish(1, p, par)
                split_x0(1, p + 1)

            split_x(0, 1, 1)
            split_x(1, 1, 1)
            edge_x0()
            make_A(0, 2)
            finish(0, 0, 0)
            edge_y()
            make_A(1, 2)
            split_x0(0, 1)
            edge_z()
            evac_H(1)
            finish(1, 0, 0)
            edge_out()
            split_x0(1, 1)
            with dve.Fori(0, PAIRS // 2 - 1) as i:
                turn(i * 2 + 1, 1)
                turn(i * 2 + 2, 0)
            finish(0, PAIRS - 1, 1)
            finish(1, PAIRS - 1, 1)


_INS = ["x", "cond_512", "L0_cond_weights", "L0_cond_biases", "L0_cond_mod_w", "L0_cond_mod_b"]


def kernel(**inputs):
    import numpy as _np
    import concourse.bacc as _bacc
    from concourse import mybir as _mybir
    from concourse.bass_utils import run_bass_kernel_spmd as _run

    nc = _bacc.Bacc("TRN2", target_bir_lowering=False, num_devices=1)
    arrays, args = {}, []
    for name in _INS:
        a = _np.ascontiguousarray(inputs[name])
        arrays[f"in_{name}_dram"] = a
        args.append(nc.dram_tensor(f"in_{name}_dram", a.shape, _mybir.dt.from_np(a.dtype), kind="ExternalInput").ap())
    shape = inputs["x"].shape
    args.append(nc.dram_tensor("out_0_dram", shape, _mybir.dt.float32, kind="ExternalOutput").ap())
    modulated_conv_kernel(nc, *args)
    r = _run(nc, [arrays], core_ids=[0])
    return r.results[0]["out_0_dram"]
```

```python
from contextlib import ExitStack

import concourse.bass as bass
from concourse import mybir

F32 = mybir.dt.float32
F32R = mybir.dt.float32r
ACT = mybir.ActivationFunctionType
ALU = mybir.AluOpType
AX_X = mybir.AxisListType.X

P = 128
PASSES = ((0, 0), (0, 1), (1, 0))
BLUR = (1, 3, 3, 1)
BLURS = (1, 6, 15, 20, 15, 6, 1)
V_S0, V_A0, V_B0, V_E1, V_E2, V_D3, V_C, V_SB1, V_SB2, NVEC = range(10)


def modulated_conv_kernel(nc, x, cond, weights, biases, mod_w, mod_b, out):
    B, C, L = x.shape
    LAYERS, _, _, K = weights.shape
    STYLE = cond.shape[1]
    PAIRS = B // 2
    HALF = L // 2
    SCALE2 = 1.0 / (C * K * K)
    SCALE = float(SCALE2 ** 0.5)
    EPS = 1e-8
    BP = B + 2
    XW = L + 12
    NXS = HALF + 6
    NJ = (HALF + 4) // 2
    NM = HALF - 2
    NR, NA, NF, NH = 3, 2, 5, 7
    EDGE = 3
    NM1 = NM // 2 + 1
    CUT = EDGE + 2 * (NM1 - 1)

    ctx = ExitStack()
    with ctx:
        def sb(name, shape, dt=F32):
            return ctx.enter_context(nc.sbuf_tensor(name, shape, dt))

        def ps(name, shape):
            return ctx.enter_context(nc.psum_tensor(name, shape, F32))

        def sem(name):
            return ctx.enter_context(nc.semaphore(name))

        def per_slot(make, name, *a):
            return [make(f"{name}{s}", *a) for s in range(2)]

        ident = sb("ident", [P, P])
        wn = sb("wn", [C, LAYERS, C, K])
        mwn = sb("mwn", [P, 2, STYLE])
        cn = sb("cn", [B, STYLE])
        bn = sb("bn", [LAYERS, 2, C])
        biases2 = sb("biases2", [P, 2, LAYERS])
        mbias, bias = biases2[:, 0], biases2[:, 1]
        mwT = sb("mwT", [P, LAYERS, 2, C])
        cT = sb("cT", [P, B])
        style = sb("style", [P, LAYERS, B])
        style2 = sb("style2", [P, LAYERS, B])
        wsq = sb("wsq", [C, LAYERS, C, K])
        wsum = sb("wsum", [C, LAYERS, C])
        wsumT = sb("wsumT", [C, LAYERS, 2, C])
        dt_ = sb("dt_", [P, LAYERS, B])
        dq = sb("dq", [P, LAYERS, B])
        dr = sb("dr", [P, LAYERS, B])
        da = sb("da", [P, LAYERS, B])
        dm = sb("dm", [P, LAYERS, B])
        vec = sb("vec", [P, NVEC, BP])
        coef = sb("coef", [C, len(BLURS) + len(BLUR), 1])
        prod = sb("prod", [C, K, len(BLURS), C])
        blur1 = sb("blur1", [C, 2 * NF, C])
        blur = sb("blur", [C, 2, 6, C])
        F_st = sb("F_st", [P, NF, C])
        V_st = sb("V_st", [P, 2, P])
        V_hl = sb("V_hl", [P, 2, 2, P], F32R)
        G_mv = sb("G_mv", [P, NA, C])
        w0T = sb("w0T", [P, K, C])
        w0_st = sb("w0_st", [P, 2, P])
        sqrt_warm = sb("sqrt_warm", [P, 1])
        w0_hl = sb("w0_hl", [P, 2, 2, P], F32R)
        y_st = sb("y_st", [P, 6, C])
        z_st = sb("z_st", [P, 3, P])
        o_st = sb("o_st", [P, 3, C])
        xe = sb("xe", [C, 2, B, 8])
        xse = sb("xse", [C, 2, B, 8])
        x0e = sb("x0e", [P, 2, B, 7])
        ye = sb("ye", [P, 2, B, 6])
        ze = sb("ze", [P, 2, B, 5])
        yc = sb("yc", [P, B])
        zc = sb("zc", [P, B])
        oe = sb("oe", [C, B, 2, EDGE])
        xin = [per_slot(sb, f"xin{par}_", [P, XW]) for par in range(2)]
        xs = per_slot(sb, "xs", [P, 2, NXS], F32R)
        xr = [per_slot(sb, f"xr{par}_", [C, L]) for par in range(2)]
        x0f = per_slot(sb, "x0f", [P, 2, NJ])
        x0 = per_slot(sb, "x0", [P, 2, 2 * NJ], F32R)
        A_sb = sb("A_sb", [P, 2, NA, 2, C], F32R)
        R_sb = per_slot(sb, "R_sb", [P, NR, C])
        H_hl = sb("H_hl", [P, 2, NH, C], F32R)
        H_st = per_slot(sb, "H_st", [P, 2, NH + 1, C], F32R)
        ot = per_slot(sb, "ot", [C, L])
        p_l0 = per_slot(ps, "p_l0", [P, 2, 512])
        p_out = per_slot(ps, "p_out", [P, 512])
        p_R = ps("p_R", [P, 512])
        p_H = ps("p_H", [P, 512])

        padded = sem("padded")
        zeroed = sem("zeroed")
        ident_made = sem("ident_made")
        w_loaded = sem("w_loaded")
        mw_loaded = sem("mw_loaded")
        cond_loaded = sem("cond_loaded")
        mb_loaded = sem("mb_loaded")
        b_loaded = sem("b_loaded")
        e_loaded = sem("e_loaded")
        x_loaded = [per_slot(sem, f"x_loaded{par}_") for par in range(2)]
        put = {n: sem(f"put_{n}") for n in ("styleT", "w0T", "w2T", "wsumT", "mbias", "bias", "style", "demod",
                                            "GT", "FT", "oT", "x0e", "ye", "ze", "oe", "zc", "oc")}
        coef_made = sem("coef_made")
        blur_step = sem("blur_step")
        blurred = {n: sem(f"blurred_{n}") for n in ("1_twice", "3", "1")}
        copied = {n: sem(f"copied_{n}") for n in ("styleT", "wsumT", "w0_st", "w0h", "w0T", "G_mv", "V_st", "Vh",
                                                  "F_st", "w2T", "o_st")}
        made = {n: sem(f"made_{n}") for n in ("wsum", "style2", "dt", "s0", "vec", "V", "w0l", "y_st",
                                              "zc", "xse", "x0e", "ye", "ze", "yc", "c", "oe")}
        dve_step = sem("dve_step")
        act_step = sem("act_step")
        sqrt_done = sem("sqrt_done")
        xh_made = per_slot(sem, "xh_made")
        xl_made = per_slot(sem, "xl_made")
        xr_made = per_slot(sem, "xr_made")
        l0_done = per_slot(sem, "l0_done")
        x0_evac = per_slot(sem, "x0_evac")
        x0h_made = per_slot(sem, "x0h_made")
        x0l_made = per_slot(sem, "x0l_made")
        Ah_made = per_slot(sem, "Ah_made")
        Al_made = per_slot(sem, "Al_made")
        R_done = sem("R_done")
        R_evac = per_slot(sem, "R_evac")
        H_done = sem("H_done")
        Hh_made = sem("Hh_made")
        Hl_made = sem("Hl_made")
        H_placed = per_slot(sem, "H_placed")
        main_done = per_slot(sem, "main_done")
        out_made = per_slot(sem, "out_made")
        edge_put = per_slot(sem, "edge_put")
        stored = per_slot(sem, "stored")

        def wait(eng, s, value):
            if not isinstance(value, int) or value > 0:
                eng.wait_ge(s, value)

        def col(v, n, lo=0, hi=P):
            return vec[lo:hi, v, bass.ds(n, 1)]

        block = ctx.enter_context(nc.Block())

        @block.gpsimd
        def _(pool):
            pool.memset(ident[:], 0.0).then_inc(zeroed, 1)
            pool.wait_ge(zeroed, 1)
            pool.affine_select(out=ident[:], in_=ident[:], compare_op=ALU.not_equal, fill=1.0, base=0,
                               pattern=[[-1, P]], channel_multiplier=1).then_inc(ident_made, 1)
            for j, v in enumerate(BLURS + BLUR):
                pool.memset(coef[:, j], float(v)).then_inc(coef_made, 1)
            for t in (blur1, blur, z_st, xe, x0e, ye, ze):
                pool.memset(t[:], 0.0).then_inc(zeroed, 1)
            count = 8
            for s in range(2):
                for rows, block in ((slice(0, C), NH), (slice(C, P), 0)):
                    pool.wait_ge(zeroed, count)
                    pool.memset(H_st[s][rows, :, block, :].bitcast(F32), 0.0).then_inc(zeroed, 1)
                    count += 1
            pool.wait_ge(zeroed, count)
            pool.wait_ge(w_loaded, 16)
            pool.wait_ge(coef_made, len(BLURS + BLUR))
            n_step = 0
            for dst, layer, j0, n, name in ((blur1[:], 1, 0, len(BLURS), "1_twice"),
                                            (blur[:, 1], 3, len(BLURS), len(BLUR), "3"),
                                            (blur[:, 0], 1, len(BLURS), len(BLUR), "1")):
                for k in range(K):
                    pool.tensor_tensor(prod[:, k, 0:n], wn[:, layer, :, k].unsqueeze(1).to_broadcast([C, n, C]),
                                       coef[:, j0:j0 + n].to_broadcast([C, n, C]), ALU.mult).then_inc(blur_step, 1)
                    n_step += 1
                for k in range(K):
                    pool.wait_ge(blur_step, n_step)
                    pool.tensor_tensor(dst[:, k:k + n], dst[:, k:k + n], prod[:, k, 0:n], ALU.add)\
                        .then_inc(blurred[name] if k == K - 1 else blur_step, 1)
                    n_step += k < K - 1
                pool.wait_ge(blurred[name], 1)
                if name == "1_twice":
                    pool.wait_ge(made["s0"], 1)
                    pool.wait_ge(e_loaded, 32)
                    for side in range(2):
                        pool.tensor_tensor(xse[:, side], xe[:, side],
                                           vec[0:C, V_S0, 0:B].unsqueeze(2).to_broadcast([C, B, 8]), ALU.mult)\
                            .then_inc(made["xse"], 1)
            pool.wait_ge(made["oe"], 1)

            def put_edges(p):
                for s in range(2):
                    wait(pool, stored[s], 16 * p)
                    n = p * 2 + s
                    pool.tensor_copy(ot[s][:, 0:EDGE], oe[:, bass.ds(n, 1), 0, :].rearrange("c a n -> c (a n)"))\
                        .then_inc(edge_put[s], 1)
                    pool.tensor_copy(ot[s][:, L - EDGE:L], oe[:, bass.ds(n, 1), 1, :].rearrange("c a n -> c (a n)"))\
                        .then_inc(edge_put[s], 1)

            put_edges(0)
            with pool.Fori(1, PAIRS) as p:
                put_edges(p)

        @block.sync
        def _(sp):
            sp.dma_start(wn[:], weights.rearrange("l o i k -> o l i k")).then_inc(w_loaded, 16)
            sp.dma_start(mwn[:], mod_w.rearrange("(t l) c s -> (l c) t s", t=2)).then_inc(mw_loaded, 16)
            sp.dma_start(cn[:], cond).then_inc(cond_loaded, 16)
            sp.dma_start(bn[:, 0, :], mod_b).then_inc(mb_loaded, 16)

            def load(s, p, par):
                n = p * 2 + s
                wait(sp, xl_made[s], p - 1)
                wait(sp, xr_made[s], p - 1)
                src = x[bass.ds(n, 1), :, :].rearrange("a c l -> (a c) l")
                sp.dma_start(xin[par][s][0:C, 2:2 + L], src).then_inc(x_loaded[par][s], 16)
                sp.dma_start(xin[par][s][C:P, 1:1 + L], src).then_inc(x_loaded[par][s], 16)

            def place_H(p):
                wait(sp, Hl_made, p + 1)
                wait(sp, main_done[1], p)
                sp.dma_start(H_st[1][0:C, :, 0:NH, :].bitcast(F32), H_hl[C:P].bitcast(F32)).then_inc(H_placed[1], 16)
                sp.dma_start(H_st[1][C:P, :, 1:NH + 1, :].bitcast(F32), H_hl[C:P].bitcast(F32))\
                  .then_inc(H_placed[1], 16)

            def store(s, p):
                n = p * 2 + s
                wait(sp, out_made[s], 2 * (p + 1))
                wait(sp, edge_put[s], 2 * (p + 1))
                dst = out[bass.ds(n, 1), :, :].rearrange("a c l -> (a c) l")
                sp.dma_start(dst, ot[s][:]).then_inc(stored[s], 16)

            sp.wait_ge(padded, 8)
            load(0, 0, 0)
            sp.dma_start(bn[:, 1, :], biases).then_inc(b_loaded, 16)
            load(1, 0, 0)
            load(0, 1, 1)
            load(1, 1, 1)
            sp.wait_ge(zeroed, 5)
            sp.dma_start(xe[:, 0, :, 1:8], x[:, :, 0:7].rearrange("b c n -> c b n")).then_inc(e_loaded, 16)
            sp.dma_start(xe[:, 1, :, 0:7], x[:, :, L - 7:L].rearrange("b c n -> c b n")).then_inc(e_loaded, 16)
            place_H(0)

            def turn(p, par):
                load(0, p + 2, par)
                store(0, p)
                load(1, p + 2, par)
                place_H(p + 1)
                store(1, p)

            load(0, 2, 0)
            load(1, 2, 0)
            place_H(1)
            store(0, 0)
            store(1, 0)
            turn(1, 1)
            with sp.Fori(1, PAIRS // 2 - 1) as i:
                turn(i * 2, 0)
                turn(i * 2 + 1, 1)
            p = PAIRS - 2
            store(0, p)
            place_H(p + 1)
            store(1, p)
            store(0, p + 1)
            sp.wait_ge(edge_put[1], 2 * PAIRS)
            for part, cols in enumerate((slice(0, CUT), slice(CUT, L))):
                sp.wait_ge(out_made[1], 2 * (PAIRS + part))
                sp.dma_start(out[B - 1, :, cols], ot[1][:, cols]).then_inc(stored[1], 16)
            sp.wait_ge(stored[0], 16 * PAIRS)
            sp.wait_ge(stored[1], 16 * (PAIRS + 1))

        @block.tensor
        def _(pe):
            def taps_transposed(l, c0):
                for k in range(K):
                    for h in range(2):
                        ins = pe.matmul(p_out[0][h * C:(h + 1) * C, c0 + k * C:c0 + (k + 1) * C], wn[:, l, :, k],
                                        ident[0:C, 0:C], start=True, stop=True)
                return ins

            def biases_down(j, bank):
                for h in range(2):
                    ins = pe.matmul(bank[h * C:(h + 1) * C, 0:LAYERS], bn[:, j, :], ident[0:LAYERS, 0:LAYERS],
                                    start=True, stop=True)
                return ins

            pe.wait_ge(ident_made, 1)
            pe.wait_ge(w_loaded, 16)
            taps_transposed(0, 0).then_inc(put["w0T"], 1)
            pe.wait_ge(mw_loaded, 16)
            pe.wait_ge(cond_loaded, 16)
            for t in range(2):
                pe.transpose(p_l0[0][:, 0, t * P:(t + 1) * P], mwn[:, t, :], ident[:])
            pe.transpose(p_l0[0][:, 0, 2 * P:2 * P + B], cn[:], ident[0:B, 0:B]).then_inc(put["styleT"], 1)
            pe.wait_ge(mb_loaded, 16)
            biases_down(0, p_R).then_inc(put["mbias"], 1)
            pe.wait_ge(made["wsum"], 1)
            for l in range(LAYERS):
                ins = pe.transpose(p_l0[1][0:C, 0, l * C:(l + 1) * C], wsum[:, l, :], ident[0:C, 0:C])
            ins.then_inc(put["wsumT"], 1)
            pe.wait_ge(copied["styleT"], 1)
            for l in range(LAYERS):
                ins = pe.matmul(p_l0[0][:, 1, l * B:(l + 1) * B], mwT[:, l].rearrange("p a c -> p (a c)"), cT[:],
                                start=True, stop=True)
            ins.then_inc(put["style"], 1)
            pe.wait_ge(zeroed, 2)
            for h, block, k in ((0, 0, 2), (1, 0, None), (0, 1, 0), (1, 1, 1)):
                c0 = block * C
                ins = pe.matmul(p_out[1][h * C:(h + 1) * C, c0:c0 + C], wn[:, 3, :, 0 if k is None else k],
                                blur1[:, 2 * NF - 1] if k is None else ident[0:C, 0:C], start=True, stop=True)
            ins.then_inc(put["GT"], 1)
            pe.wait_ge(b_loaded, 16)
            biases_down(1, p_H).then_inc(put["bias"], 1)
            pe.wait_ge(copied["wsumT"], 1)
            pe.wait_ge(made["style2"], 1)
            for l in range(LAYERS):
                ins = pe.matmul(p_l0[1][:, 1, l * B:(l + 1) * B], wsumT[:, l].rearrange("p a c -> p (a c)"),
                                style2[0:C, l, :], start=True, stop=True)
            ins.then_inc(put["demod"], 1)

            def compose_R(p):
                for s in range(2):
                    wait(pe, Al_made[s], p + 1)
                    wait(pe, R_evac[s], p)
                for q, (a, b) in enumerate(PASSES):
                    for st in range(2):
                        ins = pe.matmul(p_R[:, st * 2 * C:(st + NA) * 2 * C], V_hl[:, a, st, :],
                                        A_sb[:, b].rearrange("p a s c -> p (a s c)"),
                                        start=(q == 0 and st == 0), stop=(q == 2 and st == 1),
                                        skip_group_check=True)
                ins.then_inc(R_done, 1)

            def compose_H(p):
                wait(pe, Hl_made, p)
                wait(pe, R_evac[0], p + 1)
                wait(pe, R_evac[1], p + 1)
                for c in range(NF):
                    for s in range(2):
                        ins = pe.matmul(p_H[s * C:(s + 1) * C, c * C:(c + NR) * C], F_st[:, c, :],
                                        R_sb[s][:].rearrange("p a c -> p (a c)"), start=(c == 0), stop=(c == NF - 1),
                                        skip_group_check=True)
                ins.then_inc(H_done, 1)

            def layer0(s, p):
                wait(pe, xl_made[s], p + 1)
                wait(pe, x0_evac[s], p)
                for bank in range(2):
                    for q, (a, b) in enumerate(PASSES):
                        for st in range(2):
                            e0 = bank * NJ + st
                            ins = pe.matmul(p_l0[s][:, bank, 0:NJ], w0_hl[:, a, st, :], xs[s][:, b, e0:e0 + NJ],
                                            start=(q == 0 and st == 0), stop=(q == 2 and st == 1))
                ins.then_inc(l0_done[s], 1)

            def main(s, p, m0=0, n=NM, bank=None):
                bank = p_out[s] if bank is None else bank
                if s == 0:
                    wait(pe, H_placed[0], 2 * (p + 1))
                else:
                    wait(pe, H_placed[1], 32 * (p + 1))
                wait(pe, x0l_made[s], p + 1)
                wait(pe, out_made[s], 2 * p)
                for q, (a, b) in enumerate(PASSES):
                    for t in range(4):
                        blk = NH - 1 - 2 * t
                        ins = pe.matmul(bank[:, 0:n],
                                        H_st[s][:, a, blk:blk + 2, :].rearrange("p a c -> p (a c)"),
                                        x0[s][:, b, m0 + t:m0 + t + n], start=(q == 0 and t == 0),
                                        stop=(q == 2 and t == 3))
                ins.then_inc(main_done[s], 1)

            pe.wait_ge(made["w0l"], 1)
            pe.wait_ge(made["style2"], 1)
            pe.wait_ge(copied["styleT"], 1)
            layer0(0, 0)
            pe.wait_ge(made["dt"], 1)
            layer0(1, 0)
            pe.wait_ge(made["vec"], 1)
            pe.wait_ge(blurred["1_twice"], 1)
            for m in range(NF):
                ins = pe.transpose(p_H[:, m * C:(m + 1) * C],
                                   blur1[:, 2 * m:2 * m + 2, :].rearrange("p t i -> p (t i)"), ident[0:C, 0:C])
            ins.then_inc(put["FT"], 1)
            pe.wait_ge(copied["w0T"], 1)
            taps_transposed(2, K * C).then_inc(put["w2T"], 1)
            pe.wait_ge(made["V"], 1)
            compose_R(0)
            pe.wait_ge(copied["w2T"], 1)
            pe.wait_ge(made["yc"], 1)
            for k in range(3):
                ins = pe.matmul(p_out[0][:, 0:B], z_st[:, k, :], yc[:], start=(k == 0), stop=(k == 2))
            ins.then_inc(put["zc"], 1)
            pe.wait_ge(copied["F_st"], 1)
            compose_H(0)
            pe.wait_ge(blurred["3"], 1)
            pe.wait_ge(copied["G_mv"], 1)
            for m in range(3):
                ins = pe.transpose(p_out[1][:, (NA + m) * C:(NA + m + 1) * C],
                                   blur[:, 1, 2 * m:2 * m + 2, :].rearrange("p t i -> p (t i)"), ident[0:C, 0:C])
            ins.then_inc(put["oT"], 1)
            compose_R(1)
            pe.wait_ge(made["zc"], 1)
            pe.wait_ge(copied["o_st"], 1)
            for k in range(3):
                ins = pe.matmul(p_out[1][0:C, 0:B], o_st[:, k, :], zc[:], start=(k == 0), stop=(k == 2))
            ins.then_inc(put["oc"], 1)
            layer0(0, 1)
            pe.wait_ge(zeroed, 12)

            p_e = p_l0[1][:, 0]

            def edge_x0():
                pe.wait_ge(made["xse"], 2)
                pe.wait_ge(x0_evac[1], 1)
                for k in range(K):
                    for side in range(2):
                        ins = pe.matmul(p_e[side * C:(side + 1) * C, 0:B * 6], w0T[0:C, k, :],
                                        xse[:, side, :, k:k + 6], start=(k == 0), stop=(k == K - 1),
                                        skip_group_check=True)
                ins.then_inc(put["x0e"], 1)

            def edge_y():
                pe.wait_ge(made["x0e"], 1)
                pe.wait_ge(made["y_st"], 1)
                for k, rows in ((0, P), (2, C)):
                    c = 4 - 2 * k
                    ins = pe.matmul(p_e[:, 0:2 * B * 5], y_st[0:rows, c:c + 2, :].rearrange("p a c -> p (a c)"),
                                    x0e[0:rows, :, :, k:k + 5], start=(k == 0), stop=(k == 2))
                ins.then_inc(put["ye"], 1)

            def edge_z():
                pe.wait_ge(made["ye"], 1)
                pe.wait_ge(Hl_made, 2)
                for k in range(3):
                    ins = pe.matmul(p_H[:, 0:2 * B * 4], z_st[:, k, :], ye[:, :, :, k:k + 4],
                                    start=(k == 0), stop=(k == 2))
                ins.then_inc(put["ze"], 1)

            def edge_out():
                pe.wait_ge(made["ze"], 1)
                for k in range(3):
                    for side in range(2):
                        ins = pe.matmul(p_H[side * C:(side + 1) * C, 0:B * EDGE], o_st[:, k, :],
                                        ze[:, side, :, k:k + EDGE], start=(k == 0), stop=(k == 2),
                                        skip_group_check=True)
                ins.then_inc(put["oe"], 1)

            def turn(p):
                main(0, p)
                compose_R(p + 1)
                layer0(0, p + 1)
                compose_H(p + 1)
                main(1, p)
                layer0(1, p + 1)

            edge_x0()
            main(0, 0)
            edge_y()
            compose_H(1)
            pe.wait_ge(made["c"], 1)
            main(1, 0)
            edge_z()
            layer0(1, 1)
            edge_out()
            with pe.Fori(1, PAIRS - 1) as p:
                turn(p)
            main(0, PAIRS - 1)
            main(1, PAIRS - 1, 0, NM1, p_out[1])
            main(1, PAIRS - 1, NM - NM1, NM1, p_l0[1][:, 0])

        @block.scalar
        def _(act):
            def copy(o, a, signal=act_step):
                act.activation(o, a, ACT.Copy).then_inc(signal, 1)

            act.wait_ge(padded, 1)
            act.activation(sqrt_warm[:], xin[0][0][:, 0:1], ACT.Sqrt)
            act.wait_ge(put["styleT"], 1)
            copy(cT[:], p_l0[0][:, 0, 2 * P:2 * P + B])
            for h in range(2):
                copy(mwT[:, :, h, :], p_l0[0][:, 0, 0:2 * P].rearrange("p (l c) -> p l c", c=C),
                     copied["styleT"] if h else act_step)
            act.wait_ge(put["wsumT"], 1)
            for h in range(2):
                copy(wsumT[:, :, h, :], p_l0[1][0:C, 0, 0:LAYERS * C].rearrange("p (l c) -> p l c", c=C),
                     copied["wsumT"] if h else act_step)
            act.wait_ge(padded, 9)
            act.wait_ge(put["w0T"], 1)
            wT = p_out[0][:, 0:3 * C].rearrange("p (k c) -> p k c", c=C)
            copy(w0_st[0:C, 0, 0:C], wT[0:C, 0])
            copy(w0_st[C:P, 0, 0:C], wT[C:P, 1])
            copy(w0_st[C:P, 0, C:P], wT[C:P, 0])
            copy(w0_st[0:C, 1, 0:C], wT[0:C, 2])
            copy(w0_st[0:C, 1, C:P], wT[0:C, 1])
            copy(w0_st[C:P, 1, C:P], wT[C:P, 2], copied["w0_st"])
            act.wait_ge(copied["w0_st"], 1)
            copy(w0_hl[:, 0], w0_st[:], copied["w0h"])
            copy(w0T[:], wT, copied["w0T"])

            def split_x(s, p, par, use):
                wait(act, x_loaded[par][s], 32 * (use + 1))
                wait(act, l0_done[s], p)
                act.activation(xs[s][:, 0, 0:NXS - 1], xin[par][s][:, 0:2 * NXS - 2:2], ACT.Copy,
                               scale=col(V_S0, p * 2 + s)).then_inc(xh_made[s], 1)

            def make_A(s, p):
                wait(act, R_done, p)
                act.activation(A_sb[:, 0, :, s], G_mv[:], ACT.Copy, scale=col(V_E2, p * 2 + s))\
                   .then_inc(Ah_made[s], 1)

            def evac_R(s, p):
                wait(act, R_done, p + 1)
                wait(act, H_done, p)
                act.activation(R_sb[s][:], p_R[:, 0:NR * 2 * C].rearrange("p (a s c) -> p a s c", s=2, c=C)[:, :, s],
                               ACT.Copy, scale=col(V_E1, p * 2 + s)).then_inc(R_evac[s], 1)

            def evac_x0(s, p):
                wait(act, l0_done[s], p + 1)
                wait(act, x0l_made[s], p)
                n = p * 2 + s
                act.activation(x0f[s][:], p_l0[s][:, :, 0:NJ], ACT.Identity, scale=col(V_A0, n),
                               bias=col(V_B0, n)).then_inc(x0_evac[s], 1)

            def evac_H(p):
                wait(act, H_done, p + 1)
                wait(act, H_placed[0], 2 * p)
                wait(act, H_placed[1], 32 * p)
                act.activation(H_hl[:, 0], p_H[:, 0:NH * C].rearrange("p (a c) -> p a c", c=C), ACT.Copy)\
                   .then_inc(Hh_made, 1)

            def residual(s, p, par):
                wait(act, out_made[s], 2 * (p - 1))
                act.activation(xr[par][s][:], xin[par][s][0:C, 2:2 + L], ACT.Identity,
                               bias=col(V_C, p * 2 + s, 0, C))\
                   .then_inc(xr_made[s], 1)

            act.wait_ge(made["s0"], 1)
            split_x(0, 0, 0, 0)
            split_x(1, 0, 0, 0)
            act.wait_ge(put["GT"], 1)
            copy(G_mv[:], p_out[1][:, 0:NA * C].rearrange("p (a c) -> p a c", c=C), copied["G_mv"])
            act.wait_ge(w_loaded, 16)
            act.wait_ge(padded, 11)
            V = [wn[:, 2, :, K - 1 - b] for b in range(K)]
            copy(V_st[0:C, 0, 0:C], V[0])
            copy(V_st[C:P, 0, 0:C], V[1])
            copy(V_st[C:P, 0, C:P], V[0])
            copy(V_st[0:C, 1, 0:C], V[2])
            copy(V_st[0:C, 1, C:P], V[1])
            copy(V_st[C:P, 1, C:P], V[2], copied["V_st"])
            act.wait_ge(made["dt"], 1)
            act.activation(dq[:], dt_[:], ACT.Sqrt).then_inc(sqrt_done, 1)
            act.wait_ge(copied["V_st"], 1)
            copy(V_hl[:, 0], V_st[:], copied["Vh"])
            act.wait_ge(made["vec"], 1)
            act.wait_ge(copied["G_mv"], 1)
            make_A(0, 0)
            make_A(1, 0)
            evac_x0(0, 0)
            act.wait_ge(put["FT"], 1)
            act.activation(F_st[:], p_H[:, 0:NF * C].rearrange("p (a c) -> p a c", c=C), ACT.Copy,
                           scale=1.0 / 32).then_inc(copied["F_st"], 1)
            act.wait_ge(zeroed, 4)
            act.wait_ge(put["w2T"], 1)
            w2T = p_out[0][:, 3 * C:6 * C].rearrange("p (k c) -> p k c", c=C)
            copy(z_st[C:P, 0, 0:C], w2T[C:P, 0])
            copy(z_st[0:C, 1, 0:C], w2T[0:C, 1])
            copy(z_st[0:C, 1, C:P], w2T[0:C, 0])
            copy(z_st[C:P, 1, 0:C], w2T[C:P, 2])
            copy(z_st[C:P, 1, C:P], w2T[C:P, 1])
            copy(z_st[0:C, 2, C:P], w2T[0:C, 2], copied["w2T"])
            evac_R(0, 0)
            evac_R(1, 0)
            make_A(0, 1)
            make_A(1, 1)
            evac_x0(1, 0)
            split_x(0, 1, 1, 0)
            evac_H(0)
            act.wait_ge(put["oT"], 1)
            act.activation(o_st[:], p_out[1][:, NA * C:(NA + 3) * C].rearrange("p (a c) -> p a c", c=C), ACT.Copy,
                           scale=0.125).then_inc(copied["o_st"], 1)
            evac_R(0, 1)
            evac_R(1, 1)
            make_A(0, 2)
            make_A(1, 2)
            evac_x0(0, 1)
            split_x(1, 1, 1, 0)
            act.wait_ge(made["c"], 1)
            residual(0, 0, 0)
            residual(1, 0, 0)
            evac_H(1)
            residual(0, 1, 1)
            residual(1, 1, 1)
            evac_x0(1, 1)

            def turn(p, par, use):
                split_x(0, p + 1, 1 - par, use)
                evac_R(0, p + 1)
                evac_R(1, p + 1)
                make_A(0, p + 2)
                make_A(1, p + 2)
                evac_x0(0, p + 1)
                split_x(1, p + 1, 1 - par, use)
                residual(0, p + 1, 1 - par)
                evac_H(p + 1)
                residual(1, p + 1, 1 - par)
                evac_x0(1, p + 1)

            with act.Fori(0, PAIRS // 2 - 1) as i:
                turn(i * 2 + 1, 1, i + 1)
                turn(i * 2 + 2, 0, i + 1)

        @block.vector
        def _(dve):
            n_step = [0]

            def step(ins, name=None):
                if name:
                    ins.then_inc(made[name], 1)
                    last[0] = (made[name], 1)
                else:
                    n_step[0] += 1
                    ins.then_inc(dve_step, 1)
                    last[0] = (dve_step, n_step[0])

            last = [None]

            def then():
                dve.wait_ge(*last[0])

            def tt(o, a, b, op, name=None):
                step(dve.tensor_tensor(o, a, b, op), name)

            def ts(o, a, s1, s2=None, op0=ALU.mult, op1=ALU.bypass, name=None):
                if s2 is None:
                    step(dve.tensor_scalar(o, a, s1, None, op0), name)
                else:
                    step(dve.tensor_scalar(o, a, s1, s2, op0, op1), name)

            def stt(o, a, s1, b, op0, op1, name=None):
                step(dve.scalar_tensor_tensor(out=o, in0=a, scalar=s1, in1=b, op0=op0, op1=op1), name)

            for par in range(2):
                for s in range(2):
                    dve.memset(xin[par][s][:, 0:2], 0.0).then_inc(padded, 1)
                    dve.memset(xin[par][s][:, L:XW], 0.0).then_inc(padded, 1)
            for t in (w0_st, vec, V_st):
                dve.memset(t[:], 0.0).then_inc(padded, 1)
            dve.wait_ge(w_loaded, 16)
            tt(wsq[:], wn[:], wn[:], ALU.mult)
            then()
            step(dve.tensor_reduce(wsum[:], wsq[:], AX_X, ALU.add), "wsum")
            dve.wait_ge(put["mbias"], 1)
            ts(mbias, p_R[:, 0:LAYERS], 1.0)
            then()
            dve.wait_ge(put["style"], 1)
            dve.wait_ge(padded, 10)
            tt(style[:], p_l0[0][:, 1, 0:LAYERS * B].rearrange("p (l b) -> p l b", b=B),
               mbias.unsqueeze(2).to_broadcast([P, LAYERS, B]), ALU.add)
            then()
            ts(vec[:, V_S0, 0:B], style[:, 0, :], 1.0, name="s0")
            tt(style2[:], style[:], style[:], ALU.mult, "style2")

            def make_A(s, p):
                wait(dve, Ah_made[s], p + 1)
                dve.scalar_tensor_tensor(out=A_sb[:, 1, :, s], in0=G_mv[:], scalar=col(V_E2, p * 2 + s),
                                         in1=A_sb[:, 0, :, s].bitcast(F32), op0=ALU.mult, op1=ALU.subtract)\
                    .then_inc(Al_made[s], 1)

            def split_x(s, p, par):
                wait(dve, xh_made[s], p + 1)
                dve.scalar_tensor_tensor(out=xs[s][:, 1, 0:NXS - 1], in0=xin[par][s][:, 0:2 * NXS - 2:2],
                                         scalar=col(V_S0, p * 2 + s), in1=xs[s][:, 0, 0:NXS - 1].bitcast(F32),
                                         op0=ALU.mult, op1=ALU.subtract).then_inc(xl_made[s], 1)

            def split_x0(s, p):
                wait(dve, x0_evac[s], p + 1)
                wait(dve, main_done[s], p)
                src = x0f[s][:].rearrange("p a j -> p (a j)")
                dve.tensor_copy(x0[s][:, 0, :], src).then_inc(x0h_made[s], 1)
                dve.wait_ge(x0h_made[s], p + 1)
                dve.tensor_tensor(x0[s][:, 1, :], src, x0[s][:, 0, :].bitcast(F32), ALU.subtract)\
                    .then_inc(x0l_made[s], 1)

            def evac_H(p):
                wait(dve, Hh_made, p + 1)
                dve.tensor_tensor(H_hl[:, 1], p_H[:, 0:NH * C].rearrange("p (a c) -> p a c", c=C),
                                  H_hl[:, 0].bitcast(F32), ALU.subtract).then_inc(Hl_made, 1)
                dve.wait_ge(Hl_made, p + 1)
                wait(dve, main_done[0], p)
                for h in range(2):
                    dve.tensor_copy(H_st[0][h * C:(h + 1) * C, :, h:h + NH, :], H_hl[0:C].bitcast(F32))\
                       .then_inc(H_placed[0], 1)

            def finish(s, p, par, bank=None, m_done=0, i0=0, i1=NM - 1, part=0):
                wait(dve, main_done[s], p + 1 + part)
                wait(dve, xr_made[s], p + 1)
                wait(dve, stored[s], 16 * p)
                n = p * 2 + s
                bank = p_out[s] if bank is None else bank
                for h, m0, c0 in ((0, 1, EDGE + 1), (1, 0, EDGE)):
                    cols = slice(c0 + 2 * i0, c0 + 2 * i1 - 1, 2)
                    dve.scalar_tensor_tensor(out=ot[s][:, cols],
                                             in0=bank[h * C:(h + 1) * C, m0 + i0 - m_done:m0 + i1 - m_done],
                                             scalar=col(V_D3, n, h * C, (h + 1) * C), in1=xr[par][s][:, cols],
                                             op0=ALU.mult, op1=ALU.add).then_inc(out_made[s], 1)

            dve.wait_ge(copied["w0h"], 1)
            tt(w0_hl[:, 1], w0_st[:], w0_hl[:, 0].bitcast(F32), ALU.subtract, "w0l")
            split_x(0, 0, 0)
            dve.wait_ge(put["demod"], 1)
            ts(dt_[:], p_l0[1][:, 1, 0:LAYERS * B].rearrange("p (l b) -> p l b", b=B), SCALE2, EPS,
               ALU.mult, ALU.add, "dt")
            dve.wait_ge(put["bias"], 1)
            ts(bias, p_H[:, 0:LAYERS], 1.0)
            split_x(1, 0, 0)
            dve.wait_ge(sqrt_done, 1)
            step(dve.reciprocal(dr[:], dq[:]))
            then()
            tt(da[:], dr[:], dr[:], ALU.mult)
            then()
            tt(da[:], da[:], dt_[:], ALU.mult)
            then()
            ts(da[:], da[:], -0.5 * SCALE, 1.5 * SCALE, ALU.mult, ALU.add)
            then()
            tt(dm[:], dr[:], da[:], ALU.mult)
            then()
            tt(vec[:, V_E2, 0:B], style[:, 3, :], dm[:, 2, :], ALU.mult)
            tt(vec[:, V_E1, 0:B], style[:, 2, :], style[:, 1, :], ALU.mult)
            tt(vec[:, V_A0, 0:B], dm[:, 1, :], dm[:, 0, :], ALU.mult)
            ts(vec[:, V_B0, 0:B], dm[:, 1, :], bias[:, 0:1], name="vec")
            dve.wait_ge(copied["Vh"], 1)
            tt(V_hl[:, 1], V_st[:], V_hl[:, 0].bitcast(F32), ALU.subtract, "V")
            make_A(0, 0)
            make_A(1, 0)
            ts(vec[:, V_D3, 0:B], dm[:, 3, :], 1.0)
            ts(vec[:, V_SB1, 0:B], style[:, 2, :], bias[:, 1:2])
            ts(vec[:, V_SB2, 0:B], style[:, 3, :], bias[:, 2:3])
            then()
            ts(yc[:], vec[:, V_SB1, 0:B], 2.0, name="yc")
            split_x0(0, 0)
            dve.wait_ge(put["zc"], 1)
            tt(zc[:], p_out[0][:, 0:B], vec[:, V_E2, 0:B], ALU.mult)
            then()
            tt(zc[:], zc[:], vec[:, V_SB2, 0:B], ALU.add, "zc")
            make_A(0, 1)
            make_A(1, 1)
            split_x0(1, 0)

            def bc(v, rows, width):
                return vec[rows, v, 0:B].unsqueeze(2).to_broadcast([rows.stop - rows.start, B, width])

            lo, all_ = slice(0, C), slice(0, P)
            split_x(0, 1, 1)
            evac_H(0)
            dve.wait_ge(put["oc"], 1)
            tt(vec[0:C, V_C, 0:B], p_out[1][0:C, 0:B], vec[0:C, V_D3, 0:B], ALU.mult)
            then()
            ts(vec[0:C, V_C, 0:B], vec[0:C, V_C, 0:B], bias[0:C, 3:4], op0=ALU.add, name="c")
            dve.wait_ge(blurred["1"], 1)
            ts(y_st[0:C], blur[:, 0], 0.25)
            ts(y_st[C:P, 2:6], blur[:, 0, 0:4], 0.25, name="y_st")
            dve.wait_ge(zeroed, 8)

            def edge(dst, src, rows, width, scale, offset, name, times=1.0):
                d = [dst[:, side, :, 1 - side:1 - side + width] for side in range(2)]
                for side in range(2):
                    tt(d[side], src(side, width), bc(scale, rows, width), ALU.mult)
                then()
                for side in range(2):
                    stt(d[side], bc(offset, rows, width), times, d[side], ALU.mult, ALU.add,
                        name if side and name else None)

            def one_after_the_other(bank):
                return lambda side, width: bank[:, side * B * width:(side + 1) * B * width]\
                    .rearrange("p (b n) -> p b n", n=width)

            def one_below_the_other(bank):
                return lambda side, width: bank[side * C:(side + 1) * C, 0:B * width]\
                    .rearrange("p (b n) -> p b n", n=width)

            p_e = p_l0[1][:, 0]

            def edge_x0():
                dve.wait_ge(put["x0e"], 1)
                edge(x0e[0:C], one_below_the_other(p_e), lo, 6, V_A0, V_B0, None)
                then()
                ts(x0e[C:P, :, :, 0:6], x0e[0:C, :, :, 1:7], 1.0, name="x0e")

            def edge_y():
                dve.wait_ge(put["ye"], 1)
                edge(ye, one_after_the_other(p_e), all_, 5, V_E1, V_SB1, None, 2.0)
                then()
                stt(ye[0:C, 0, :, 1], vec[0:C, V_SB1, 0:B], -0.25, ye[0:C, 0, :, 1], ALU.mult, ALU.add)
                stt(ye[C:P, 1, :, 4], vec[C:P, V_SB1, 0:B], -0.25, ye[C:P, 1, :, 4], ALU.mult, ALU.add, "ye")

            def edge_z():
                dve.wait_ge(put["ze"], 1)
                edge(ze, one_after_the_other(p_H), all_, 4, V_E2, V_SB2, "ze")

            def edge_out():
                dve.wait_ge(put["oe"], 1)
                for op in range(3):
                    for side in range(2):
                        d = oe[:, :, side, :]
                        if op == 0:
                            tt(d, one_below_the_other(p_H)(side, EDGE), bc(V_D3, lo, EDGE), ALU.mult)
                        elif op == 1:
                            ts(d, d, bias[0:C, 3:4], op0=ALU.add)
                        else:
                            first = 4 if side else 1
                            tt(d, d, xe[:, side, :, first:first + EDGE], ALU.add, "oe" if side else None)
                    if op < 2:
                        then()

            def turn(p, par):
                split_x(0, p + 1, 1 - par)
                finish(0, p, par)
                make_A(0, p + 2)
                make_A(1, p + 2)
                split_x(1, p + 1, 1 - par)
                split_x0(0, p + 1)
                evac_H(p + 1)
                finish(1, p, par)
                split_x0(1, p + 1)

            edge_x0()
            make_A(0, 2)
            make_A(1, 2)
            split_x(1, 1, 1)
            finish(0, 0, 0)
            edge_y()
            split_x0(0, 1)
            evac_H(1)
            finish(1, 0, 0)
            edge_z()
            edge_out()
            split_x0(1, 1)
            with dve.Fori(0, PAIRS // 2 - 1) as i:
                turn(i * 2 + 1, 1)
                turn(i * 2 + 2, 0)
            finish(0, PAIRS - 1, 1)
            finish(1, PAIRS - 1, 1, i1=NM1 - 1)
            finish(1, PAIRS - 1, 1, p_l0[1][:, 0], m_done=NM - NM1, i0=NM1 - 1, part=1)


_INS = ["x", "cond_512", "L0_cond_weights", "L0_cond_biases", "L0_cond_mod_w", "L0_cond_mod_b"]


def kernel(**inputs):
    import numpy as _np
    import concourse.bacc as _bacc
    from concourse import mybir as _mybir
    from concourse.bass_utils import run_bass_kernel_spmd as _run

    nc = _bacc.Bacc("TRN2", target_bir_lowering=False, num_devices=1)
    arrays, args = {}, []
    for name in _INS:
        a = _np.ascontiguousarray(inputs[name])
        arrays[f"in_{name}_dram"] = a
        args.append(nc.dram_tensor(f"in_{name}_dram", a.shape, _mybir.dt.from_np(a.dtype), kind="ExternalInput").ap())
    shape = inputs["x"].shape
    args.append(nc.dram_tensor("out_0_dram", shape, _mybir.dt.float32, kind="ExternalOutput").ap())
    modulated_conv_kernel(nc, *args)
    r = _run(nc, [arrays], core_ids=[0])
    return r.results[0]["out_0_dram"]
```
